# Optimizing a Trainium2 kernel written in Bass

```python
import numpy as np
import jax
import jax.numpy as jnp

def _softmax(x, axis=-1):
    return jax.nn.softmax(x, axis=axis)

def _gelu(x):
    return jax.nn.gelu(x, approximate=True)

def _silu(x):
    return jax.nn.silu(x)

def _sigmoid(x):
    return jax.nn.sigmoid(x)

def _layernorm(x, axis=-1, eps=1e-05):
    m = jnp.mean(x, axis=axis, keepdims=True)
    v = jnp.var(x, axis=axis, keepdims=True)
    return (x - m) / jnp.sqrt(v + eps)

def _scatter_add(tgt, idx, src, axis=0):
    return tgt.at[idx].add(src)

def _segment_sum(src, seg, n):
    return jax.ops.segment_sum(src, seg, n)
kernel_name = 'mk_gnn_preln_d2_gnn_r8_3ab9ff'

def setup_inputs(seed: int=0):
    np.random.seed(seed)
    _w = jnp.asarray

    def _rec_inputs():
        import jax
        import jax.numpy as jnp
        _gk = jax.random.key(seed)
        x = -0.000202 + 1 * jax.random.normal(jax.random.fold_in(_gk, 1), (12500, 64), jnp.float32)
        src = jax.random.randint(jax.random.fold_in(_gk, 2), (400000,), 0, 12500, jnp.int32)
        dst = jax.random.randint(jax.random.fold_in(_gk, 3), (400000,), 0, 12500, jnp.int32)
        _o = jnp.argsort(dst, stable=True)
        src = src[_o]
        dst = dst[_o]
        edge_attr_64 = -5.16925e-05 + 1.00005 * jax.random.normal(jax.random.fold_in(_gk, 13), (400000, 64), jnp.float32)
        edge_weight = jax.random.uniform(jax.random.fold_in(_gk, 15), (400000,), jnp.float32, 0.0, 0.999999)
        return (x, src, dst, edge_attr_64, edge_weight)
    x, src, dst, edge_attr_64, edge_weight = _rec_inputs()

    def _L0_gnn_setup():
        import jax, jax.numpy as jnp
        import numpy as np
        N_NODES = 12500
        N_EDGES = 150000
        D_IN = 64
        D_OUT = 64
        key = jax.random.key(seed)
        k_x, k_src, k_dst, k_w, k_W, k_b = jax.random.split(key, 6)
        x = jax.random.normal(k_x, (N_NODES, D_IN), dtype=jnp.float32)
        edge_src = jax.random.randint(k_src, (N_EDGES,), 0, N_NODES, dtype=jnp.int32)
        edge_dst = jax.random.randint(k_dst, (N_EDGES,), 0, N_NODES, dtype=jnp.int32)
        edge_w = jax.random.uniform(k_w, (N_EDGES,), dtype=jnp.float32)
        bound = 1.0 / np.sqrt(D_IN)
        W = jax.random.uniform(k_W, (D_IN, D_OUT), minval=-bound, maxval=bound, dtype=jnp.float32)
        b = jax.random.uniform(k_b, (D_OUT,), minval=-bound, maxval=bound, dtype=jnp.float32)
        return {'x': x, 'W': W, 'b': b, 'edge_src': edge_src, 'edge_dst': edge_dst, 'edge_w': edge_w}
    _L0_gnn_all = _L0_gnn_setup()
    _L0_gnn_in = {k: v for k, v in _L0_gnn_all.items() if k in ('W', 'b')}
    del _L0_gnn_all

    def _L1_gnn_setup():
        import jax, jax.numpy as jnp
        import numpy as np
        N_NODES = 12500
        N_EDGES = 200000
        N_GRAPHS = 512
        D = 64
        BN_EPS = 1e-05

        def _batchnorm(h, gamma, beta):
            mean = jnp.mean(h, axis=0)
            var = jnp.var(h, axis=0)
            return (h - mean) * jax.lax.rsqrt(var + BN_EPS) * gamma + beta
        key = jax.random.key(seed)
        ks = jax.random.split(key, 16)
        x = jax.random.normal(ks[0], (N_NODES, D), dtype=jnp.float32)
        edge_index = jax.random.randint(ks[1], (2, N_EDGES), 0, N_NODES, dtype=jnp.int64)
        edge_attr = jax.random.normal(ks[2], (N_EDGES, D), dtype=jnp.float32)
        global_attr = jax.random.normal(ks[3], (N_GRAPHS, D), dtype=jnp.float32)
        batch = jnp.sort(jax.random.randint(ks[4], (N_NODES,), 0, N_GRAPHS, dtype=jnp.int64))
        W1 = jax.random.normal(ks[5], (3 * D, D), dtype=jnp.float32) / np.sqrt(3 * D)
        b1 = jnp.zeros((D,), dtype=jnp.float32)
        W2 = jax.random.normal(ks[6], (D, D), dtype=jnp.float32) / np.sqrt(D)
        b2 = jnp.zeros((D,), dtype=jnp.float32)
        W3 = jax.random.normal(ks[7], (D, D), dtype=jnp.float32) / np.sqrt(D)
        b3 = jnp.zeros((D,), dtype=jnp.float32)
        g1 = jnp.ones((D,), dtype=jnp.float32)
        bt1 = jnp.zeros((D,), dtype=jnp.float32)
        g2 = jnp.ones((D,), dtype=jnp.float32)
        bt2 = jnp.zeros((D,), dtype=jnp.float32)
        g3 = jnp.ones((D,), dtype=jnp.float32)
        bt3 = jnp.zeros((D,), dtype=jnp.float32)
        return dict(x=x, edge_index=edge_index, edge_attr=edge_attr, global_attr=global_attr, batch=batch, W1=W1, b1=b1, W2=W2, b2=b2, W3=W3, b3=b3, g1=g1, bt1=bt1, g2=g2, bt2=bt2, g3=g3, bt3=bt3)
    _L1_gnn_all = _L1_gnn_setup()
    _L1_gnn_in = {k: v for k, v in _L1_gnn_all.items() if k in ('global_attr', 'W1', 'b1', 'W2', 'b2', 'W3', 'b3', 'g1', 'bt1', 'g2', 'bt2', 'g3', 'bt3')}
    del _L1_gnn_all
    return {'x': x, 'src': src, 'dst': dst, 'edge_attr_64': edge_attr_64, 'edge_weight': edge_weight, 'L0_gnn_W': _L0_gnn_in['W'], 'L0_gnn_b': _L0_gnn_in['b'], 'L1_gnn_global_attr': _L1_gnn_in['global_attr'], 'L1_gnn_W1': _L1_gnn_in['W1'], 'L1_gnn_b1': _L1_gnn_in['b1'], 'L1_gnn_W2': _L1_gnn_in['W2'], 'L1_gnn_b2': _L1_gnn_in['b2'], 'L1_gnn_W3': _L1_gnn_in['W3'], 'L1_gnn_b3': _L1_gnn_in['b3'], 'L1_gnn_g1': _L1_gnn_in['g1'], 'L1_gnn_bt1': _L1_gnn_in['bt1'], 'L1_gnn_g2': _L1_gnn_in['g2'], 'L1_gnn_bt2': _L1_gnn_in['bt2'], 'L1_gnn_g3': _L1_gnn_in['g3'], 'L1_gnn_bt3': _L1_gnn_in['bt3']}

def reference(x, src, dst, edge_attr_64, edge_weight, L0_gnn_W, L0_gnn_b, L1_gnn_global_attr, L1_gnn_W1, L1_gnn_b1, L1_gnn_W2, L1_gnn_b2, L1_gnn_W3, L1_gnn_b3, L1_gnn_g1, L1_gnn_bt1, L1_gnn_g2, L1_gnn_bt2, L1_gnn_g3, L1_gnn_bt3):
    import jax
    import jax.numpy as jnp

    def _L0_gnn_ref(x, W, b, edge_src, edge_dst, edge_w):
        import jax, jax.numpy as jnp
        import numpy as np
        N_NODES = 12500
        N_EDGES = 150000
        D_IN = 64
        D_OUT = 64
        h = jnp.dot(x, W) + b
        msgs = edge_w[:, None] * h[edge_src]
        out = jax.ops.segment_sum(msgs, edge_dst, num_segments=N_NODES)
        return out

    def _L1_gnn_ref(x, edge_index, edge_attr, global_attr, batch, W1, b1, W2, b2, W3, b3, g1, bt1, g2, bt2, g3, bt3):
        import jax, jax.numpy as jnp
        import numpy as np
        N_NODES = 12500
        N_EDGES = 200000
        N_GRAPHS = 512
        D = 64
        BN_EPS = 1e-05

        def _batchnorm(h, gamma, beta):
            mean = jnp.mean(h, axis=0)
            var = jnp.var(h, axis=0)
            return (h - mean) * jax.lax.rsqrt(var + BN_EPS) * gamma + beta
        src = edge_index[0]
        sums = jax.ops.segment_sum(edge_attr, src, num_segments=N_NODES)
        counts = jax.ops.segment_sum(jnp.ones((edge_attr.shape[0],), edge_attr.dtype), src, num_segments=N_NODES)
        v_e = sums / jnp.maximum(counts, 1.0)[:, None]
        comb = jnp.concatenate([x, v_e, global_attr[batch]], axis=1)
        out = _batchnorm(jax.nn.relu(comb @ W1 + b1), g1, bt1)
        out = _batchnorm(jax.nn.relu(out @ W2 + b2), g2, bt2)
        out = _batchnorm(jax.nn.relu(out @ W3 + b3), g3, bt3)
        return out
    edge_index = jnp.stack([src, dst])
    batch0 = jnp.zeros((12500,), jnp.int32)
    h = jnp.maximum(_layernorm(x, axis=-1), 0.0)
    x = x + _L0_gnn_ref(h, L0_gnn_W, L0_gnn_b, src, dst, edge_weight)
    h = jnp.maximum(_layernorm(x, axis=-1), 0.0)
    x = x + _L1_gnn_ref(h, edge_index, edge_attr_64, L1_gnn_global_attr, batch0, L1_gnn_W1, L1_gnn_b1, L1_gnn_W2, L1_gnn_b2, L1_gnn_W3, L1_gnn_b3, L1_gnn_g1, L1_gnn_bt1, L1_gnn_g2, L1_gnn_bt2, L1_gnn_g3, L1_gnn_bt3)
    return x

_drawn_inputs = setup_inputs


def setup_inputs(seed=0):
    import zlib

    import numpy as np

    out = dict(_drawn_inputs(seed))
    spreads = {'L1_gnn_b1': (0.0, 0.1),
     'L1_gnn_b2': (0.0, 0.309),
     'L1_gnn_b3': (0.0, 0.509),
     'L1_gnn_g1': (1.0, 0.2),
     'L1_gnn_bt1': (0.0, 0.342),
     'L1_gnn_g2': (1.0, 0.2),
     'L1_gnn_bt2': (0.0, 0.571),
     'L1_gnn_g3': (1.0, 0.2),
     'L1_gnn_bt3': (0.0, 0.284)}
    factors = {}
    for name, (base, spread) in spreads.items():
        noise = np.random.default_rng([zlib.crc32(name.encode()), seed]).standard_normal(out[name].shape)
        drawn = base * np.exp(spread * noise) if base else spread * noise
        out[name] = jnp.asarray(drawn.astype(out[name].dtype))
    for name, factor in factors.items():
        out[name] = (out[name] * factor).astype(out[name].dtype)
    return out
```

```python
import concourse.bass as bass
from concourse import mybir
from contextlib import ExitStack

N = 12500
E = 400000
D = 64
P = 128
B = -(-N // P)
LAST = N - (B - 1) * P
NPAD = B * P
T = 25
CH = P * T
C = E // CH
G = 5
GT = T // G
K = GT
R = NPAD + P
NG = 7
GB = B // NG
GC = GB * D
GP = GB // 2
COLS = B // 2 * P
BAD = P - LAST
HALF = GC // 2
EPS = 1e-5
assert C * CH == E and C % 2 == 1 and B % (2 * NG) == 0 and T % K == 0


def gnn_kernel(nc, x, src, dst, ea, ew, w0, b0, gattr, w1, b1, w2, b2, w3, b3, g1, bt1, g2, bt2, g3, bt3, out):
    f32, bf16, i32 = mybir.dt.float32, mybir.dt.bfloat16, mybir.dt.int32
    ALU, ACT, AX = mybir.AluOpType, mybir.ActivationFunctionType, mybir.AxisListType
    ds = bass.ds

    src_v = src.rearrange("(c t) -> c t", t=T)
    dst_v = dst.rearrange("(c t) -> c t", t=T)
    ew_v = ew.rearrange("(c t) -> c t", t=T)
    ea_v = ea.rearrange("(c t) d -> c (t d)", t=T)
    dst_chunks = dst.rearrange("(c e) -> c e", e=CH)

    h_tab = nc.dram_tensor("h_tab", [P, B * D], f32).ap()
    h_rows = h_tab.rearrange("p (b d) -> (p b) d", d=D)
    sum_tab = nc.dram_tensor("sum_tab", [K * R, D], f32).ap()
    span_d = nc.dram_tensor("span_d", [C, 4], i32).ap()
    base_d = nc.dram_tensor("base_d", [C, 1], f32).ap()

    ctx = ExitStack()
    with ctx:
        def sb(name, shape, dt=f32):
            return ctx.enter_context(nc.sbuf_tensor(name, shape, dt))

        def sem(name):
            return ctx.enter_context(nc.semaphore(name))

        X = sb("X", [P, B * D])
        acc = sb("acc", [P, (B + 1) * D])
        Rl = sb("Rl", [P, COLS])
        ea_s = sb("ea_s", [P, 2, T * D])
        gat = sb("gat", [P, 2, T * D])
        ust = sb("ust", [P, 2, T * D])
        src_i = sb("src_i", [P, 2, T], i32)
        dst_i = sb("dst_i", [P, 2, T], i32)
        ew_s = sb("ew_s", [P, 2, T])
        gidx = sb("gidx", [P, 2, T], i32)
        sidx = sb("sidx", [P, 2, T], i32)
        hi_i = sb("hi_i", [P, T], i32)
        lo_i = sb("lo_i", [P, T], i32)
        hi_f = sb("hi_f", [P, T])
        lo_f = sb("lo_f", [P, T])
        src_f = sb("src_f", [P, T])
        row_f = sb("row_f", [P, T])
        flag = sb("flag", [P, T])
        parts = sb("parts", [P, P], bf16)
        partsT = sb("partsT", [2 * T, P], bf16)
        pw_s = sb("pw_s", [P, T])
        Mt = sb("Mt", [P, 2, GT * P])
        oh_lo = sb("oh_lo", [P, 2, GT * P], bf16)
        oh_hi = sb("oh_hi", [P, 2, GT * B], bf16)
        drel = sb("drel", [P, T])
        St = sb("St", [P, G, GT * P])
        cnt = sb("cnt", [P, B])
        iota_i = sb("iota_i", [P, P], i32)
        iota_f = sb("iota_f", [P, P])
        iota_b = sb("iota_b", [P, P], bf16)
        mod_i = sb("mod_i", [P, P], i32)
        mod_f = sb("mod_f", [P, P])
        pid_i = sb("pid_i", [P, 1], i32)
        pid_f = sb("pid_f", [P, 1])
        pmod_i = sb("pmod_i", [P, 1], i32)
        pmod_f = sb("pmod_f", [P, 1])
        kmod = sb("kmod", [P, 1])
        spare_row = sb("spare_row", [P, 1])
        ident = sb("ident", [P, P])
        ident_b = sb("ident_b", [P, P], bf16)
        fold = sb("fold", [P, P])
        before = sb("before", [P, P])
        sel_i = sb("sel_i", [2 * T, T * P], i32)
        sel = sb("sel", [2 * T, T * P], bf16)
        pw_i = sb("pw_i", [P, 1], i32)
        pw_b = sb("pw_b", [P, 1], i32)
        pw_f = pw_b[:, :].bitcast(f32)
        thr = sb("thr", [P, 1])
        dst_all = ust[:, :, :].rearrange("p a b -> p (a b)")[0:C, 0:CH].bitcast(i32)
        mm_i = sb("mm_i", [P, 2], i32)
        mm_f = sb("mm_f", [P, 1])
        mm_s = sb("mm_s", [P, 2], i32)
        span_f = sb("span_f", [P, 4])
        span_i = sb("span_i", [P, 4], i32)
        base_f = sb("base_f", [P, 1])
        spans = sb("spans", [1, C * 4], i32)
        bases = sb("bases", [P, C])
        Wd = sb("Wd", [P, 5, P])
        w1c = sb("w1c", [D, P])
        gcol = sb("gcol", [D, 1])
        brow = sb("brow", [P, D])
        vecs = sb("vecs", [P, 9])
        Ws = sb("Ws", [P, P])
        hg = sb("hg", [P, GC])
        xc = sb("xc", [P, GC])
        sq = sb("sq", [P, GC])
        ve = sb("ve", [P, GC])
        hT = sb("hT", [P, 2, GC])
        tg = sb("tg", [P, K, GC])
        ln_s = sb("ln_s", [P, GB])
        ln_m = sb("ln_m", [P, GB])
        ln_v = sb("ln_v", [P, GB])
        ln_r = sb("ln_r", [P, GB])
        eps_t = sb("eps_t", [P, 1])
        rc = sb("rc", [P, B])
        st = sb("st", [P, 16])
        bias = sb("bias", [P, 3])

        PS = ctx.enter_context(nc.psum_tensor("PS", [P, 8 * 512], f32))

        def bank(n, width, parts_n=P):
            return PS[0:parts_n, n * 512:n * 512 + width]

        bc_ps = [bank(0, GT * P), bank(2, GT * P)]
        u_ps = [bank(4, GT * D), bank(5, GT * D)]
        pw_ps = [PS[:, n * 512 + GT * D:n * 512 + GT * D + GT] for n in (4, 5)]
        win_ps = bank(6, D)
        cnt_ps = bank(7, B)
        ptT_ps = PS[:, 7 * 512 + 128:7 * 512 + 192].bitcast(bf16)
        T_ps = [PS[:, j * 128:(j + 1) * 128] for j in range(GP)]
        T_all = PS[:, 0:GC]
        V_ps = [PS[:, 1024 + j * 128:1024 + (j + 1) * 128] for j in range(GP)]
        V_all = PS[:, 1024:1024 + GC]
        Z_ps = [bank(4, HALF), bank(5, HALF)]
        small_ps = bank(6, 8)

        s_in = sem("inputs_loaded")
        s_w = sem("weights_loaded")
        s_da = sem("dst_loaded")
        s_zero = sem("zeros_ready")
        s_tabz = sem("tables_zeroed")
        s_iota = sem("iotas_ready")
        s_const = sem("constants_ready")
        s_sp = sem("spans_in_sbuf")
        s_spo = sem("spans_stored")
        s_spl = sem("spans_loaded")
        s_nw = sem("window_counts_ready")
        s_cum = sem("windows_summed")
        s_xc = sem("centred")
        s_sq = sem("squared")
        s_var = sem("variance_ready")
        s_std = sem("deviation_ready")
        s_h = sem("h_ready")
        s_hTp = sem("h_transposed")
        s_hTs = sem("h_transposed_in_sbuf")
        s_Hp = sem("h_table_product")
        s_Hs = sem("h_table_rows_in_sbuf")
        s_Ho = [sem("h_table_stored_even"), sem("h_table_stored_odd")]
        s_ldA = [sem("edges_loaded_even"), sem("edges_loaded_odd")]
        s_ldB = [sem("dst_weights_loaded_even"), sem("dst_weights_loaded_odd")]
        s_parts = sem("src_parts_ready")
        s_pT = sem("src_parts_transposed")
        s_pTs = sem("src_parts_transposed_in_sbuf")
        s_gidx = sem("gather_rows_ready")
        s_bc = sem("src_broadcast")
        s_M = sem("masks_ready")
        s_U = sem("duplicates_summed")
        s_Us = sem("sums_in_sbuf")
        s_oh = sem("one_hots_ready")
        s_cm = sem("counts_product")
        s_cu = sem("counts_taken")
        s_sidx = sem("scatter_rows_ready")
        s_pace = sem("pool_passed_a_wait")
        s_free = sem("scatter_slots_free")
        s_g = [sem("gathered_even"), sem("gathered_odd")]
        s_tab = [sem(f"table_{k}_added") for k in range(K)]
        s_S = sem("window_one_hots_ready")
        s_Sm = sem("window_product")
        s_acc = sem("window_taken")
        s_win = sem("chunk_windows_done")
        s_tg = sem("table_group_loaded")
        s_v = sem("mean_edges_ready")
        s_vTp = sem("mean_edges_transposed")
        s_vTs = sem("mean_edges_transposed_in_sbuf")
        s_z = sem("layer_product")
        s_r = sem("layer_activated")
        s_sum = sem("layer_summed")
        s_tot = sem("layer_total")
        s_mean = sem("layer_mean")
        s_dev = sem("layer_deviations")
        s_vp = sem("layer_deviations_summed")
        s_vt = sem("layer_variance_total")
        s_vs = sem("layer_variance")
        s_sd = sem("layer_std")
        s_bn = sem("norm_ready")
        s_bp = sem("next_bias_product")
        s_wr = sem("next_weights_ready")
        s_b1 = sem("first_bias_ready")
        s_y = sem("normed_ready")
        s_yT = sem("normed_transposed")
        s_o = sem("out_rows_ready")
        s_out = [sem("out_stored_even"), sem("out_stored_odd")]

        block = ctx.enter_context(nc.Block())

        @block.sync
        def _(sp):
            sp.dma_start(dst_all, dst_chunks).then_inc(s_da, 16)
            sp.wait_ge(s_zero, 1)
            sp.dma_start(X[:, 0:(B - 1) * D].rearrange("p (b d) -> p b d", d=D),
                         x[0:(B - 1) * P, :].rearrange("(b p) d -> p b d", p=P)).then_inc(s_in, 16)
            sp.dma_start(X[0:LAST, (B - 1) * D:B * D], x[(B - 1) * P:N, :]).then_inc(s_in, 16)
            for n, w in enumerate((w0, w1[0:D, :], w1[D:2 * D, :], w2, w3)):
                for o in (0, D):
                    sp.dma_start(Wd[o:o + D, n, o:o + D], w).then_inc(s_w, 16)
            with nc.allow_non_contiguous_dma(reason="columns of 64 values"):
                for n, v in enumerate((b1, b2, b3, g1, g2, g3, bt1, bt2, bt3)):
                    for o in (0, D):
                        sp.dma_start(vecs[o:o + D, n:n + 1], v.rearrange("(d o) -> d o", o=1)).then_inc(s_w, 16)
                sp.dma_start(gcol[:, :], gattr[0:1, :].rearrange("o d -> d o")).then_inc(s_w, 16)
            for o in (0, D):
                sp.dma_start(w1c[:, o:o + D], w1[2 * D:3 * D, :]).then_inc(s_w, 16)
            sp.dma_start(brow[:, :], b0.rearrange("(o d) -> o d", o=1).broadcast_to([P, D])).then_inc(s_w, 16)

            def load_edges(c, q):
                rows = ds(c * P, P)
                sp.dma_start(src_i[:, q, :], src_v[rows, :]).then_inc(s_ldA[q], 16)
                sp.dma_start(ea_s[:, q, :], ea_v[rows, :]).then_inc(s_ldA[q], 16)

            def load_dst(c, q):
                rows = ds(c * P, P)
                sp.dma_start(dst_i[:, q, :], dst_v[rows, :]).then_inc(s_ldB[q], 16)
                sp.dma_start(ew_s[:, q, :], ew_v[rows, :]).then_inc(s_ldB[q], 16)

            load_edges(0, 0)
            load_dst(0, 0)
            sp.wait_ge(s_sp, 1)
            sp.dma_start(span_d, span_i[0:C, :]).then_inc(s_spo, 16)
            sp.dma_start(base_d, base_f[0:C, :]).then_inc(s_spo, 16)
            sp.wait_ge(s_spo, 32)
            sp.dma_start(spans[:, :], span_d.rearrange("(o c) f -> o (c f)", o=1)).then_inc(s_spl, 16)
            with nc.allow_non_contiguous_dma(reason="one row for all partitions"):
                sp.dma_start(bases[:, :], base_d.rearrange("(o c) f -> o (c f)", o=1).broadcast_to([P, C])).then_inc(s_spl, 16)
            for i in range(NG):
                sp.wait_ge(s_Hs, i + 1)
                sp.dma_start(h_tab[:, i * GC:(i + 1) * GC], tg[:, i % 2, :]).then_inc(s_Ho[i % 2], 16)

            def load_chunk(c, q):
                sp.wait_ge(s_sidx, c)
                load_edges(c, q)
                sp.wait_ge(s_win, c + 1)
                load_dst(c, q)

            with sp.Fori(0, (C - 1) // 2) as i:
                load_chunk(2 * i + 1, 1)
                load_chunk(2 * i + 2, 0)

            for k in range(K):
                sp.wait_ge(s_tab[k], 16 * G * C)
            tabs = sum_tab.rearrange("(k r) d -> k (r d)", k=K)[:, 0:NPAD * D].rearrange("k (p b d) -> p k (b d)", p=P, b=B)

            def load_tables(i):
                for k in range(K):
                    sp.dma_start(tg[:, k, :], tabs[:, k, ds(i * GC, GC)]).then_inc(s_tg, 16)

            load_tables(0)
            with sp.Fori(1, NG) as i:
                sp.wait_ge(s_v, i)
                load_tables(i)
            o_v = out[0:(B - 1) * P, :].rearrange("(b p) d -> p b d", p=P)
            for i in range(NG):
                sp.wait_ge(s_o, i + 1)
                rows = tg[:, i % 2, :].rearrange("p (b d) -> p b d", d=D)
                nb = GB if i < NG - 1 else GB - 1
                sp.dma_start(o_v[:, i * GB:i * GB + nb, :], rows[:, 0:nb, :]).then_inc(s_out[i % 2], 16)
            sp.dma_start(out[(B - 1) * P:N, :], tg[0:LAST, (NG - 1) % 2, GC - D:GC]).then_inc(s_out[(NG - 1) % 2], 16)
            sp.wait_ge(s_out[0], 16 * 5)
            sp.wait_ge(s_out[1], 16 * 3)

        @block.gpsimd
        def _(pool):
            nc.gpsimd.iota(iota_i[:, :], pattern=[[1, P]], base=0, channel_multiplier=0)
            nc.gpsimd.iota(pid_i[:, :], pattern=[[0, 1]], base=0, channel_multiplier=1)
            nc.gpsimd.iota(pw_i[:, :], pattern=[[0, 1]], base=190, channel_multiplier=-1)
            nc.gpsimd.iota(sel_i[:, :], pattern=[[1, T], [0, P]], base=0, channel_multiplier=0).then_inc(s_iota, 1)
            pool.wait_ge(s_zero, 1)
            for k in range(K):
                pool.dma_start(sum_tab[k * R:(k + 1) * R, :].rearrange("(p b) d -> p (b d)", p=P),
                               acc[:, :]).then_inc(s_tabz, 16)
            pool.wait_ge(s_tabz, 16 * K)

            def scatter(c, q, first=False):
                pool.wait_ge(s_sidx, c + 1)
                pool.wait_ge(s_Us, G * (c + 1) + 2)
                for t in range(T):
                    k, g = t % K, t // K
                    if not (first and g == 0):
                        pool.wait_ge(s_tab[k], 16 * (G * c + g))
                        pool.sem_inc(s_pace, 1)
                    pool.indirect_dma_start(
                        out=sum_tab, out_offset=bass.IndirectOffsetOnAxis(ap=sidx[:, q, t:t + 1], axis=0),
                        in_=ust[:, q, t * D:(t + 1) * D], in_offset=None,
                        element_offset=k * R * D, compute_op=ALU.add).then_inc(s_tab[k], 16)
                    if t == K - 1 and not first:
                        pool.sem_inc(s_free, 1)

            def gather(c, q):
                pool.wait_ge(s_gidx, c + 1)
                pool.wait_ge(s_win, c + 1)
                pool.sem_inc(s_pace, 1)
                for t in range(T):
                    pool.indirect_dma_start(
                        out=gat[:, q, t * D:(t + 1) * D], out_offset=None, in_=h_rows,
                        in_offset=bass.IndirectOffsetOnAxis(ap=gidx[:, q, t:t + 1], axis=0)).then_inc(s_g[q], 16)

            scatter(0, 0, first=True)
            pool.wait_ge(s_Ho[0], 16 * 4)
            pool.wait_ge(s_Ho[1], 16 * 3)
            with pool.Fori(0, (C - 1) // 2) as i:
                gather(2 * i, 0)
                scatter(2 * i + 1, 1)
                gather(2 * i + 1, 1)
                scatter(2 * i + 2, 0)
            gather(C - 1, 0)

        @block.scalar
        def _(act):
            act.wait_ge(s_const, 1)

            def squares(n):
                act.wait_ge(s_xc, n + 1)
                nc.scalar.activation(sq[:, :], xc[:, :], ACT.Square).then_inc(s_sq, 1)
                act.wait_ge(s_var, n + 1)
                nc.scalar.activation(ln_r[:, :], ln_v[:, :], ACT.Sqrt, bias=eps_t[:, :], scale=1.0 / D).then_inc(s_std, 1)

            with act.Fori(0, NG) as i:
                squares(i)
                act.wait_ge(s_hTp, i + 1)
                nc.scalar.copy(hT[:, 0, :], T_all).then_inc(s_hTs, 1)

            def stage(c, q):
                act.wait_ge(s_free, c + 1)
                for g in range(G):
                    b = (q + g) % 2
                    act.wait_ge(s_U, G * c + g + 3)
                    nc.scalar.copy(ust[:, q, g * GT * D:(g + 1) * GT * D], u_ps[b])
                    nc.scalar.copy(pw_s[:, g * GT:(g + 1) * GT], pw_ps[b]).then_inc(s_Us, 1)

            stage(0, 0)
            with act.Fori(0, (C - 1) // 2) as i:
                stage(2 * i + 1, 1)
                stage(2 * i + 2, 0)

            act.wait_ge(s_b1, 1)
            with act.Fori(0, NG) as i:
                squares(i + NG)
                act.wait_ge(s_hTp, i + NG + 1)
                nc.scalar.copy(hT[:, 0, :], T_all).then_inc(s_hTs, 1)
                act.wait_ge(s_vTp, i + 1)
                nc.scalar.copy(hT[:, 1, :], V_all).then_inc(s_vTs, 1)
                for h in range(2):
                    act.wait_ge(s_z, 2 * i + h + 1)
                    nc.scalar.activation(Rl[:, ds(i * GC + h * HALF, HALF)], Z_ps[h], ACT.Relu,
                                         bias=bias[:, 0:1]).then_inc(s_r, 1)
            for n in range(3):
                if n:
                    act.wait_ge(s_wr, n)
                    with act.Fori(0, NG) as i:
                        for h in range(2):
                            act.wait_ge(s_z, 2 * NG * n + 2 * i + h + 1)
                            nc.scalar.activation(Rl[:, ds(i * GC + h * HALF, HALF)], Z_ps[h], ACT.Relu,
                                                 bias=bias[:, n:n + 1]).then_inc(s_r, 1)
                act.wait_ge(s_mean, n + 1)
                nc.scalar.activation(acc[:, 0:COLS - BAD], Rl[:, 0:COLS - BAD], ACT.Square, bias=st[:, 2:3],
                                     accum_out=st[:, 3:4])
                nc.scalar.activation(acc[0:D, COLS - BAD:COLS], Rl[0:D, COLS - BAD:COLS], ACT.Square,
                                     bias=st[0:D, 2:3], accum_out=st[0:D, 4:5]).then_inc(s_dev, 1)
                act.wait_ge(s_vs, n + 1)
                nc.scalar.activation(st[:, 7:8], st[:, 6:7], ACT.Sqrt, bias=eps_t[:, :], scale=1.0 / N).then_inc(s_sd, 1)

        @block.vector
        def _(dve):
            V = nc.vector

            def fence():
                V.drain()

            def by_block(a):
                return a.rearrange("p (b d) -> p b d", d=D)

            V.memset(acc[:, :], 0.0)
            V.memset(X[:, (B - 1) * D:B * D], 0.0)
            V.memset(Wd[:, :, :], 0.0)
            V.memset(cnt[:, :], 0.0)
            V.memset(st[:, :], 0.0)
            V.memset(parts[:, :], 0.0)
            V.memset(eps_t[:, :], EPS)
            V.drain().then_inc(s_zero, 1)
            dve.wait_ge(s_iota, 1)
            V.tensor_copy(iota_f[:, :], iota_i[:, :])
            V.tensor_copy(iota_b[:, :], iota_i[:, :])
            V.tensor_copy(pid_f[:, :], pid_i[:, :])
            V.tensor_single_scalar(mod_i[:, :], iota_i[:, :], D - 1, ALU.bitwise_and)
            V.tensor_single_scalar(pmod_i[:, :], pid_i[:, :], D - 1, ALU.bitwise_and)
            V.tensor_single_scalar(pw_b[:, :], pw_i[:, :], 23, ALU.logical_shift_left)
            fence()
            V.tensor_copy(mod_f[:, :], mod_i[:, :])
            V.tensor_copy(pmod_f[:, :], pmod_i[:, :])
            V.tensor_scalar(kmod[:, :], pid_f[:, :], float(T), -float(T), ALU.is_ge, ALU.mult)
            V.tensor_scalar(spare_row[:, :], pid_f[:, :], float(NPAD), None, ALU.add)
            V.tensor_scalar(thr[:, :], pw_f, 2.5, None, ALU.mult)
            V.tensor_scalar(ident[:, :], iota_f[:, :], pid_f[:, :], None, ALU.is_equal)
            V.tensor_scalar(ident_b[:, :], iota_f[:, :], pid_f[:, :], None, ALU.is_equal)
            V.tensor_scalar(before[:, :], iota_f[:, :], pid_f[:, :], None, ALU.is_gt)
            fence()
            V.tensor_tensor(kmod[:, :], kmod[:, :], pid_f[:, :], ALU.add)
            V.tensor_scalar(fold[:, :], mod_f[:, :], pmod_f[:, :], None, ALU.is_equal)
            fence()
            V.tensor_scalar(sel[:, :], sel_i[:, :], kmod[0:2 * T, :], None, ALU.is_equal)
            V.drain().then_inc(s_const, 1)
            V.drain().then_inc(s_U, 2)
            V.drain().then_inc(s_Us, 2)
            V.drain().then_inc(s_M, 2)
            V.drain().then_inc(s_cm, 2)
            V.drain().then_inc(s_cu, 1)
            V.drain().then_inc(s_free, 2)
            V.drain().then_inc(s_Sm, G)
            V.drain().then_inc(s_acc, 1)
            V.drain().then_inc(s_win, 2)

            dve.wait_ge(s_da, 16)
            V.tensor_reduce(mm_i[0:C, 0:1], dst_all, AX.X, ALU.min)
            V.tensor_reduce(mm_i[0:C, 1:2], dst_all, AX.X, ALU.max)
            fence()
            V.tensor_single_scalar(mm_s[0:C, :], mm_i[0:C, :], 7, ALU.arith_shift_right)
            V.memset(span_f[0:C, 3:4], 0.0)
            fence()
            V.tensor_copy(span_f[0:C, 0:1], mm_s[0:C, 0:1])
            V.tensor_copy(mm_f[0:C, :], mm_s[0:C, 1:2])
            fence()
            V.scalar_tensor_tensor(out=span_f[0:C, 1:2], in0=mm_f[0:C, :], scalar=1.0, in1=span_f[0:C, 0:1],
                                   op0=ALU.add, op1=ALU.subtract)
            V.tensor_scalar(base_f[0:C, :], span_f[0:C, 0:1], float(P), None, ALU.mult)
            V.drain().then_inc(s_nw, 1)
            dve.wait_ge(s_w, 16 * 32)
            dve.wait_ge(s_cum, 1)
            V.tensor_copy(span_f[0:C, 2:3], small_ps[0:C, 0:1])
            V.tensor_tensor(bias[:, 0:1], small_ps[:, 1:2], vecs[:, 0:1], ALU.add).then_inc(s_b1, 1)
            fence()
            V.tensor_copy(span_i[0:C, :], span_f[0:C, :]).then_inc(s_sp, 1)

            def layer_norm(n, i, second=False):
                xg = X[:, ds(i * GC, GC)]
                if second:
                    V.tensor_tensor(xg, xg, acc[:, ds(i * GC, GC)], ALU.add)
                    fence()
                V.tensor_reduce(ln_s[:, :], by_block(xg), AX.X, ALU.add)
                fence()
                V.tensor_scalar(ln_m[:, :], ln_s[:, :], 1.0 / D, None, ALU.mult)
                fence()
                V.tensor_tensor(by_block(xc[:, :]), by_block(xg), ln_m[:, :].unsqueeze(2).broadcast_to([P, GB, D]),
                                ALU.subtract).then_inc(s_xc, 1)
                dve.wait_ge(s_sq, n + 1)
                V.tensor_reduce(ln_v[:, :], by_block(sq[:, :]), AX.X, ALU.add).then_inc(s_var, 1)
                dve.wait_ge(s_std, n + 1)
                V.reciprocal(ln_m[:, :], ln_r[:, :])
                fence()
                V.scalar_tensor_tensor(out=by_block(hg[:, :]), in0=by_block(xc[:, :]), scalar=0.0,
                                       in1=ln_m[:, :].unsqueeze(2).broadcast_to([P, GB, D]),
                                       op0=ALU.max, op1=ALU.mult).then_inc(s_h, 1)

            dve.wait_ge(s_in, 32)
            for i in range(NG):
                layer_norm(i, i)
                dve.wait_ge(s_Hp, i + 1)
                if i >= 2:
                    dve.wait_ge(s_Ho[i % 2], 16 * (i // 2))
                V.tensor_tensor(by_block(tg[:, i % 2, :]), by_block(V_all),
                                brow[:, :].unsqueeze(1).broadcast_to([P, GB, D]), ALU.add).then_inc(s_Hs, 1)

            def prepare(c, q, loads):
                dve.wait_ge(s_ldA[q], loads)
                V.tensor_single_scalar(hi_i[:, :], src_i[:, q, :], 7, ALU.arith_shift_right)
                V.tensor_single_scalar(lo_i[:, :], src_i[:, q, :], P - 1, ALU.bitwise_and)
                fence()
                V.tensor_copy(hi_f[:, :], hi_i[:, :])
                V.tensor_copy(lo_f[:, :], lo_i[:, :])
                fence()
                V.tensor_scalar(parts[:, 0:T], hi_f[:, :], float(P), None, ALU.mult)
                V.tensor_copy(parts[:, T:2 * T], lo_f[:, :])
                V.scalar_tensor_tensor(out=src_f[:, :], in0=hi_f[:, :], scalar=float(P), in1=lo_f[:, :],
                                       op0=ALU.mult, op1=ALU.add)
                V.scalar_tensor_tensor(out=row_f[:, :], in0=lo_f[:, :], scalar=float(B), in1=hi_f[:, :],
                                       op0=ALU.mult, op1=ALU.add)
                V.drain().then_inc(s_parts, 1)
                V.tensor_copy(gidx[:, q, :], row_f[:, :]).then_inc(s_gidx, 1)
                dve.wait_ge(s_pT, c + 1)
                V.tensor_copy(partsT[:, :], ptT_ps[0:2 * T, :]).then_inc(s_pTs, 1)
                for g in range(G):
                    b = (q + g) % 2
                    n = G * c + g
                    dve.wait_ge(s_cm, n + 1)
                    for j in range(GT):
                        t = g * GT + j
                        V.tensor_scalar(oh_lo[:, b, j * P:(j + 1) * P], iota_b[:, :], lo_f[:, t:t + 1], None, ALU.is_equal)
                        last = V.tensor_scalar(oh_hi[:, b, j * B:(j + 1) * B], iota_b[:, 0:B], hi_f[:, t:t + 1], None,
                                               ALU.is_equal)
                    last.then_inc(s_oh, 1)
                    dve.wait_ge(s_bc, n + 1)
                    dve.wait_ge(s_U, n + 1)
                    V.tensor_tensor(Mt[:, b, :].rearrange("p (t i) -> p t i", i=P),
                                    bc_ps[b].rearrange("p (t i) -> p t i", i=P),
                                    src_f[:, g * GT:(g + 1) * GT].unsqueeze(2).broadcast_to([P, GT, P]),
                                    ALU.is_equal).then_inc(s_M, 1)
                dve.wait_ge(s_cm, G * (c + 1) + 2)
                V.tensor_tensor(cnt[:, :], cnt[:, :], cnt_ps, ALU.add).then_inc(s_cu, 1)
                dve.wait_ge(s_Us, G * (c + 1) + 2)
                V.tensor_scalar(flag[:, :], pw_s[:, :], thr[:, :], None, ALU.is_lt)
                V.tensor_scalar(row_f[:, :], row_f[:, :], spare_row[:, :], None, ALU.subtract)
                fence()
                V.tensor_tensor(row_f[:, :], row_f[:, :], flag[:, :], ALU.mult)
                fence()
                dve.wait_ge(s_free, c + 1)
                V.tensor_scalar(sidx[:, q, :], row_f[:, :], spare_row[:, :], None, ALU.add).then_inc(s_sidx, 1)

            def windows(c, q, loads):
                dve.wait_ge(s_ldB[q], loads)
                V.tensor_copy(drel[:, :], dst_i[:, q, :])
                fence()
                V.tensor_scalar(drel[:, :], drel[:, :], bases[:, ds(c, 1)], None, ALU.subtract)
                fence()
                first = dve.value_load(spans[0:1, ds(4 * c, 1)], min_val=0, max_val=B - 1)
                count = dve.value_load(spans[0:1, ds(4 * c + 1, 1)], min_val=1, max_val=B)
                done = dve.value_load(spans[0:1, ds(4 * c + 2, 1)], min_val=0, max_val=B * C)
                with dve.Fori(0, count) as j:
                    for g in range(G):
                        dve.wait_ge(s_Sm, (done + j) * G + g + 1)
                        for t in range(GT):
                            e = g * GT + t
                            last = V.tensor_scalar(St[:, g, t * P:(t + 1) * P], iota_f[:, :], drel[:, e:e + 1],
                                                   ew_s[:, q, e:e + 1], ALU.is_equal, ALU.mult)
                        last.then_inc(s_S, 1)
                    dve.wait_ge(s_Sm, (done + j) * G + 2 * G)
                    V.tensor_scalar(drel[:, :], drel[:, :], float(P), None, ALU.subtract)
                    a = acc[:, ds(nc.s_assert_within(first + j, min_val=0, max_val=B - 1) * D, D)]
                    V.tensor_tensor(a, a, win_ps, ALU.add).then_inc(s_acc, 1)
                    fence()
                V.drain().then_inc(s_win, 1)

            dve.wait_ge(s_spl, 32)
            prepare(0, 0, 32)
            with dve.Fori(0, (C - 1) // 2) as i:
                prepare(2 * i + 1, 1, 32 * i + 32)
                windows(2 * i, 0, 32 * i + 32)
                prepare(2 * i + 2, 0, 32 * i + 64)
                windows(2 * i + 1, 1, 32 * i + 32)
            windows(C - 1, 0, 32 * ((C + 1) // 2))

            V.tensor_scalar(rc[:, :], cnt[:, :], 1.0, None, ALU.max)
            fence()
            V.reciprocal(rc[:, :], rc[:, :])
            with dve.Fori(0, NG) as i:
                layer_norm(NG + i, i, second=True)
                dve.wait_ge(s_tg, 16 * K * (i + 1))
                V.tensor_tensor(sq[:, :], tg[:, 0, :], tg[:, 1, :], ALU.add)
                for k in range(2, K):
                    fence()
                    V.tensor_tensor(sq[:, :], sq[:, :], tg[:, k, :], ALU.add)
                fence()
                V.tensor_tensor(by_block(ve[:, :]), by_block(sq[:, :]),
                                rc[:, ds(i * GB, GB)].unsqueeze(2).broadcast_to([P, GB, D]), ALU.mult).then_inc(s_v, 1)

            for n in range(3):
                dve.wait_ge(s_r, 2 * NG * (n + 1))
                V.memset(Rl[D:P, COLS - BAD:COLS], 0.0)
                fence()
                V.tensor_reduce(st[:, 0:1], Rl[:, :], AX.X, ALU.add).then_inc(s_sum, 1)
                dve.wait_ge(s_tot, n + 1)
                V.tensor_scalar(st[:, 1:2], small_ps[:, 2:3], 1.0 / N, None, ALU.mult)
                V.tensor_scalar(st[:, 2:3], small_ps[:, 2:3], -1.0 / N, None, ALU.mult).then_inc(s_mean, 1)
                dve.wait_ge(s_dev, n + 1)
                V.tensor_tensor(st[:, 5:6], st[:, 3:4], st[:, 4:5], ALU.add).then_inc(s_vp, 1)
                dve.wait_ge(s_vt, n + 1)
                V.tensor_copy(st[:, 6:7], small_ps[:, 3:4]).then_inc(s_vs, 1)
                dve.wait_ge(s_sd, n + 1)
                V.reciprocal(st[:, 8:9], st[:, 7:8])
                fence()
                V.tensor_tensor(st[:, 9:10], st[:, 8:9], vecs[:, 3 + n:4 + n], ALU.mult)
                fence()
                V.tensor_tensor(st[:, 10:11], st[:, 9:10], st[:, 1:2], ALU.mult)
                fence()
                V.tensor_tensor(st[:, 11:12], vecs[:, 6 + n:7 + n], st[:, 10:11], ALU.subtract).then_inc(s_bn, 1)
                if n < 2:
                    V.tensor_scalar(Ws[:, :], Wd[:, 3 + n, :], st[:, 9:10], None, ALU.mult)
                    dve.wait_ge(s_bp, n + 1)
                    V.tensor_tensor(bias[:, n + 1:n + 2], small_ps[:, 4:5], vecs[:, n + 1:n + 2], ALU.add).then_inc(s_wr, 1)
            fence()
            for i in range(NG):
                V.tensor_scalar(hg[:, :], Rl[:, i * GC:(i + 1) * GC], st[:, 9:10], st[:, 11:12],
                                ALU.mult, ALU.add).then_inc(s_y, 1)
                dve.wait_ge(s_yT, i + 1)
                if i >= 2:
                    dve.wait_ge(s_out[i % 2], 16 * (i // 2))
                V.tensor_tensor(tg[:, i % 2, :], X[:, i * GC:(i + 1) * GC], T_all, ALU.add).then_inc(s_o, 1)

        @block.tensor
        def _(pe):
            mm = nc.tensor.matmul

            pe.wait_ge(s_const, 1)
            pe.wait_ge(s_nw, 1)
            pe.wait_ge(s_w, 16 * 32)
            mm(small_ps[0:C, 0:1], before[0:C, 0:C], span_f[0:C, 1:2], start=True, stop=True)
            mm(small_ps[:, 1:2], w1c[:, :], gcol[:, :], start=True, stop=True).then_inc(s_cum, 1)

            def transpose_h():
                for j in range(GP):
                    last = nc.tensor.transpose(T_ps[j], hg[:, j * P:(j + 1) * P], ident[:, :])
                return last

            with pe.Fori(0, NG) as i:
                pe.wait_ge(s_h, i + 1)
                transpose_h().then_inc(s_hTp, 1)
                pe.wait_ge(s_hTs, i + 1)
                for j in range(GP):
                    last = mm(V_ps[j], hT[:, 0, j * P:(j + 1) * P], Wd[:, 0, :], start=True, stop=True)
                last.then_inc(s_Hp, 1)

            def broadcast(c, q, g):
                b = (q + g) % 2
                pe.wait_ge(s_M, G * c + g + 1)
                for j in range(GT):
                    t = g * GT + j
                    last = mm(bc_ps[b][:, j * P:(j + 1) * P], sel[:, t * P:(t + 1) * P], partsT[:, :], start=True, stop=True)
                last.then_inc(s_bc, 1)

            def prepare(c, q):
                pe.wait_ge(s_parts, c + 1)
                pe.wait_ge(s_cu, c + 1)
                nc.tensor.transpose(ptT_ps, parts[:, :], ident_b[:, :]).then_inc(s_pT, 1)
                pe.wait_ge(s_pTs, c + 1)
                broadcast(c, q, 0)
                broadcast(c, q, 1)
                for g in range(G):
                    b = (q + g) % 2
                    n = G * c + g
                    pe.wait_ge(s_M, n + 3)
                    pe.wait_ge(s_Us, n + 1)
                    for j in range(GT):
                        t = g * GT + j
                        mask = Mt[:, b, j * P:(j + 1) * P]
                        mm(u_ps[b][:, j * D:(j + 1) * D], mask, ea_s[:, q, t * D:(t + 1) * D], start=True, stop=True)
                        last = mm(pw_ps[b][:, j:j + 1], mask, pw_f, start=True, stop=True)
                    last.then_inc(s_U, 1)
                    pe.wait_ge(s_oh, n + 1)
                    for j in range(GT):
                        t = g * GT + j
                        last = mm(cnt_ps, oh_lo[:, b, j * P:(j + 1) * P], oh_hi[:, b, j * B:(j + 1) * B],
                                  start=(t == 0), stop=(t == T - 1))
                    last.then_inc(s_cm, 1)
                    if g + 2 < G:
                        broadcast(c, q, g + 2)

            def windows(c, q, gathers):
                pe.wait_ge(s_g[q], gathers)
                count = pe.value_load(spans[0:1, ds(4 * c + 1, 1)], min_val=1, max_val=B)
                done = pe.value_load(spans[0:1, ds(4 * c + 2, 1)], min_val=0, max_val=B * C)
                with pe.Fori(0, count) as j:
                    pe.wait_ge(s_acc, done + j + 1)
                    for g in range(G):
                        pe.wait_ge(s_S, (done + j) * G + g + 1)
                        for t in range(GT):
                            e = g * GT + t
                            last = mm(win_ps, St[:, g, t * P:(t + 1) * P], gat[:, q, e * D:(e + 1) * D],
                                      start=(e == 0), stop=(e == T - 1))
                        last.then_inc(s_Sm, 1)

            pe.wait_ge(s_spl, 32)
            prepare(0, 0)
            with pe.Fori(0, (C - 1) // 2) as i:
                prepare(2 * i + 1, 1)
                windows(2 * i, 0, 16 * T * (i + 1))
                prepare(2 * i + 2, 0)
                windows(2 * i + 1, 1, 16 * T * (i + 1))
            windows(C - 1, 0, 16 * T * ((C + 1) // 2))

            with pe.Fori(0, NG) as i:
                pe.wait_ge(s_h, NG + i + 1)
                transpose_h().then_inc(s_hTp, 1)
                pe.wait_ge(s_v, i + 1)
                for j in range(GP):
                    last = nc.tensor.transpose(V_ps[j], ve[:, j * P:(j + 1) * P], ident[:, :])
                last.then_inc(s_vTp, 1)
                pe.wait_ge(s_hTs, NG + i + 1)
                pe.wait_ge(s_vTs, i + 1)
                for h in range(2):
                    cols = slice(h * HALF, (h + 1) * HALF)
                    mm(Z_ps[h], Wd[:, 1, :], hT[:, 0, cols], start=True, stop=False)
                    mm(Z_ps[h], Wd[:, 2, :], hT[:, 1, cols], start=False, stop=True).then_inc(s_z, 1)
            for n in range(3):
                if n:
                    pe.wait_ge(s_wr, n)
                    with pe.Fori(0, NG) as i:
                        for h in range(2):
                            pe.wait_ge(s_r, 2 * NG * n + 2 * i + h - 1)
                            mm(Z_ps[h], Ws[:, :], Rl[:, ds(i * GC + h * HALF, HALF)], start=True, stop=True).then_inc(s_z, 1)
                pe.wait_ge(s_sum, n + 1)
                mm(small_ps[:, 2:3], fold[:, :], st[:, 0:1], start=True, stop=True).then_inc(s_tot, 1)
                pe.wait_ge(s_vp, n + 1)
                mm(small_ps[:, 3:4], fold[:, :], st[:, 5:6], start=True, stop=True).then_inc(s_vt, 1)
                if n < 2:
                    pe.wait_ge(s_bn, n + 1)
                    mm(small_ps[:, 4:5], Wd[:, 3 + n, :], st[:, 11:12], start=True, stop=True).then_inc(s_bp, 1)
            with pe.Fori(0, NG) as i:
                pe.wait_ge(s_y, i + 1)
                transpose_h().then_inc(s_yT, 1)


_INS = ["x", "src", "dst", "edge_attr_64", "edge_weight", "L0_gnn_W", "L0_gnn_b", "L1_gnn_global_attr",
        "L1_gnn_W1", "L1_gnn_b1", "L1_gnn_W2", "L1_gnn_b2", "L1_gnn_W3", "L1_gnn_b3",
        "L1_gnn_g1", "L1_gnn_bt1", "L1_gnn_g2", "L1_gnn_bt2", "L1_gnn_g3", "L1_gnn_bt3"]


def kernel(**inputs):
    import numpy as np
    import concourse.bacc as bacc
    from concourse.bass_utils import run_bass_kernel_spmd

    nc = bacc.Bacc("TRN2", target_bir_lowering=False, num_devices=1)
    arrays, args = {}, []
    for name in _INS:
        a = np.ascontiguousarray(inputs[name])
        arrays[f"in_{name}"] = a
        args.append(nc.dram_tensor(f"in_{name}", a.shape, mybir.dt.from_np(a.dtype), kind="ExternalInput").ap())
    out = nc.dram_tensor("out_0", (N, D), mybir.dt.float32, kind="ExternalOutput").ap()
    gnn_kernel(nc, *args, out)
    r = run_bass_kernel_spmd(nc, [arrays], core_ids=[0])
    return r.results[0]["out_0"]
```

```python
import concourse.bass as bass
from concourse import mybir
from contextlib import ExitStack

N = 12500
E = 400000
D = 64
P = 128
B = -(-N // P)
LAST = N - (B - 1) * P
NPAD = B * P
T = 25
CH = P * T
C = E // CH
G = 5
GT = T // G
K = GT
R = NPAD + P
NG = 7
GB = B // NG
GC = GB * D
GP = GB // 2
COLS = B // 2 * P
BAD = P - LAST
HALF = GC // 2
EPS = 1e-5
assert C * CH == E and C % 2 == 1 and B % (2 * NG) == 0 and T % K == 0


def gnn_kernel(nc, x, src, dst, ea, ew, w0, b0, gattr, w1, b1, w2, b2, w3, b3, g1, bt1, g2, bt2, g3, bt3, out):
    f32, bf16, i32 = mybir.dt.float32, mybir.dt.bfloat16, mybir.dt.int32
    ALU, ACT, AX = mybir.AluOpType, mybir.ActivationFunctionType, mybir.AxisListType
    ds = bass.ds

    src_v = src.rearrange("(c t) -> c t", t=T)
    dst_v = dst.rearrange("(c t) -> c t", t=T)
    ew_v = ew.rearrange("(c t) -> c t", t=T)
    ea_v = ea.rearrange("(c t) d -> c (t d)", t=T)
    dst_chunks = dst.rearrange("(c e) -> c e", e=CH)

    h_tab = nc.dram_tensor("h_tab", [P, B * D], f32).ap()
    h_rows = h_tab.rearrange("p (b d) -> (p b) d", d=D)
    sum_tab = nc.dram_tensor("sum_tab", [K * R, D], f32).ap()
    span_d = nc.dram_tensor("span_d", [C, 4], i32).ap()
    base_d = nc.dram_tensor("base_d", [C, 1], f32).ap()

    ctx = ExitStack()
    with ctx:
        def sb(name, shape, dt=f32):
            return ctx.enter_context(nc.sbuf_tensor(name, shape, dt))

        def sem(name):
            return ctx.enter_context(nc.semaphore(name))

        X = sb("X", [P, B * D])
        acc = sb("acc", [P, (B + 1) * D])
        Rl = sb("Rl", [P, COLS])
        rows_sb = sb("rows_sb", [P, 6 * T * D])
        by_parity = rows_sb[:, :].rearrange("p (k q n) -> p k q n", k=3, q=2)
        ea_s = by_parity[:, 0]
        gat = by_parity[:, 1]
        ust = by_parity[:, 2]
        tg = rows_sb[:, 0:2 * K * GC].rearrange("p (q k n) -> p q k n", q=2, k=K)
        hrow = Rl[:, 0:2 * GC].rearrange("p (q n) -> p q n", q=2)
        src_i = sb("src_i", [P, 2, T], i32)
        dst_i = sb("dst_i", [P, 2, T], i32)
        ew_s = sb("ew_s", [P, 2, T])
        gidx = sb("gidx", [P, 2, T], i32)
        sidx = sb("sidx", [P, 2, T], i32)
        hi_i = sb("hi_i", [P, T], i32)
        lo_i = sb("lo_i", [P, T], i32)
        hi_f = sb("hi_f", [P, T])
        lo_f = sb("lo_f", [P, T])
        src_f = sb("src_f", [P, T])
        row_f = sb("row_f", [P, T])
        flag = sb("flag", [P, T])
        parts = sb("parts", [P, P], bf16)
        partsT = sb("partsT", [2 * T, P], bf16)
        pw_s = sb("pw_s", [P, T])
        Mt = sb("Mt", [P, 2, GT * P], bf16)
        oh_lo = sb("oh_lo", [P, 2, GT * P], bf16)
        oh_hi = sb("oh_hi", [P, 2, GT * B], bf16)
        drel = sb("drel", [P, T])
        St = sb("St", [P, G, GT * P], bf16)
        ea_p = sb("ea_p", [P, 3, T * D], bf16)
        msg_p = sb("msg_p", [P, T, 3, D], bf16)
        wsum = sb("wsum", [P, D])
        cnt = sb("cnt", [P, B])
        iota_i = sb("iota_i", [P, P], i32)
        iota_f = sb("iota_f", [P, P])
        iota_b = sb("iota_b", [P, P], bf16)
        mod_i = sb("mod_i", [P, P], i32)
        mod_f = sb("mod_f", [P, P])
        pid_i = sb("pid_i", [P, 1], i32)
        pid_f = sb("pid_f", [P, 1])
        pmod_i = sb("pmod_i", [P, 1], i32)
        pmod_f = sb("pmod_f", [P, 1])
        kmod = sb("kmod", [P, 1])
        spare_row = sb("spare_row", [P, 1])
        ident = sb("ident", [P, P])
        ident_b = sb("ident_b", [P, P], bf16)
        fold = sb("fold", [P, P])
        before = sb("before", [P, P])
        sel_i = Rl[0:2 * T, 0:T * P].bitcast(i32)
        sel = sb("sel", [2 * T, T * P], bf16)
        pw_i = sb("pw_i", [P, 1], i32)
        pw_b = sb("pw_b", [P, 1], i32)
        pw_h = sb("pw_h", [P, 1], bf16)
        pw_f = pw_b[:, :].bitcast(f32)
        thr = sb("thr", [P, 1])
        dst_all = rows_sb[0:C, 0:CH].bitcast(i32)
        mm_i = sb("mm_i", [P, 2], i32)
        mm_f = sb("mm_f", [P, 1])
        mm_s = sb("mm_s", [P, 2], i32)
        span_f = sb("span_f", [P, 4])
        span_i = sb("span_i", [P, 4], i32)
        base_f = sb("base_f", [P, 1])
        spans = sb("spans", [1, C * 4], i32)
        bases = sb("bases", [P, C])
        Wd = sb("Wd", [P, 5, P])
        w1c = sb("w1c", [D, P])
        gcol = sb("gcol", [D, 1])
        brow = sb("brow", [P, D])
        vecs = sb("vecs", [P, 9])
        Ws = sb("Ws", [P, P])
        hg = sb("hg", [P, 2, GC])
        xc = sb("xc", [P, 2, GC])
        sq = sb("sq", [P, 2, GC])
        tsum = sb("tsum", [P, GC])
        ve = sb("ve", [P, GC])
        hT = sb("hT", [P, 2, GC])
        ln_s = sb("ln_s", [P, GB])
        ln_m = sb("ln_m", [P, GB])
        ln_v = sb("ln_v", [P, 2, GB])
        ln_r = sb("ln_r", [P, 2, GB])
        ln_q = sb("ln_q", [P, GB])
        eps_t = sb("eps_t", [P, 1])
        rc = sb("rc", [P, B])
        st = sb("st", [P, 16])
        bias = sb("bias", [P, 3])

        PS = ctx.enter_context(nc.psum_tensor("PS", [P, 8 * 512], f32))

        def bank(n, width, parts_n=P):
            return PS[0:parts_n, n * 512:n * 512 + width]

        bc_ps = [bank(0, GT * P), bank(2, GT * P)]
        u_ps = [bank(4, GT * D), bank(5, GT * D)]
        pw_ps = [PS[:, n * 512 + GT * D:n * 512 + GT * D + GT] for n in (4, 5)]
        win_ps = bank(6, 3 * D)
        cnt_ps = bank(7, B)
        ptT_ps = PS[:, 7 * 512 + 128:7 * 512 + 192].bitcast(bf16)
        T_ps = [PS[:, j * 128:(j + 1) * 128] for j in range(GP)]
        T_all = PS[:, 0:GC]
        V_ps = [PS[:, 1024 + j * 128:1024 + (j + 1) * 128] for j in range(GP)]
        V_all = PS[:, 1024:1024 + GC]
        Z_ps = [bank(4, HALF), bank(5, HALF)]
        small_ps = bank(6, 8)

        s_in = sem("inputs_loaded")
        s_w = sem("weights_loaded")
        s_da = sem("dst_loaded")
        s_zero = sem("zeros_ready")
        s_tabz = sem("tables_zeroed")
        s_iota = sem("iotas_ready")
        s_const = sem("constants_ready")
        s_sp = sem("spans_in_sbuf")
        s_spo = sem("spans_stored")
        s_spl = sem("spans_loaded")
        s_nw = sem("window_counts_ready")
        s_cum = sem("windows_summed")
        s_xc = sem("centred")
        s_sq = sem("squared")
        s_var = sem("variance_ready")
        s_std = sem("deviation_ready")
        s_h = sem("h_ready")
        s_hTp = sem("h_transposed")
        s_hTs = sem("h_transposed_in_sbuf")
        s_Hp = sem("h_table_product")
        s_Hs = sem("h_table_rows_in_sbuf")
        s_Ho = [sem("h_table_stored_even"), sem("h_table_stored_odd")]
        s_ldA = [sem("edges_loaded_even"), sem("edges_loaded_odd")]
        s_ldB = [sem("dst_weights_loaded_even"), sem("dst_weights_loaded_odd")]
        s_parts = sem("src_parts_ready")
        s_pT = sem("src_parts_transposed")
        s_pTs = sem("src_parts_transposed_in_sbuf")
        s_gidx = sem("gather_rows_ready")
        s_er = sem("edge_parts_rounded")
        s_ed = sem("edge_rests_ready")
        s_mr = sem("message_parts_rounded")
        s_md = sem("message_rests_ready")
        s_bc = sem("src_broadcast")
        s_M = sem("masks_ready")
        s_U = sem("duplicates_summed")
        s_Us = sem("sums_in_sbuf")
        s_oh = sem("one_hots_ready")
        s_cm = sem("counts_product")
        s_cu = sem("counts_taken")
        s_sidx = sem("scatter_rows_ready")
        s_pace = sem("pool_passed_a_wait")
        s_free = sem("scatter_slots_free")
        s_g = [sem("gathered_even"), sem("gathered_odd")]
        s_tab = [sem(f"table_{k}_added") for k in range(K)]
        s_S = sem("window_one_hots_ready")
        s_Sm = sem("window_product")
        s_acc = sem("window_taken")
        s_win = sem("chunk_windows_done")
        s_tg = [sem("table_group_loaded_even"), sem("table_group_loaded_odd")]
        s_v = sem("mean_edges_ready")
        s_vTp = sem("mean_edges_transposed")
        s_vTs = sem("mean_edges_transposed_in_sbuf")
        s_z = sem("layer_product")
        s_r = sem("layer_activated")
        s_sum = sem("layer_summed")
        s_tot = sem("layer_total")
        s_mean = sem("layer_mean")
        s_dev = sem("layer_deviations")
        s_vp = sem("layer_deviations_summed")
        s_vt = sem("layer_variance_total")
        s_vs = sem("layer_variance")
        s_sd = sem("layer_std")
        s_bn = sem("norm_ready")
        s_bp = sem("next_bias_product")
        s_wr = sem("next_weights_ready")
        s_b1 = sem("first_bias_ready")
        s_y = sem("normed_ready")
        s_yT = sem("normed_transposed")
        s_o = sem("out_rows_ready")
        s_out = [sem("out_stored_even"), sem("out_stored_odd")]

        block = ctx.enter_context(nc.Block())

        @block.sync
        def _(sp):
            sp.dma_start(dst_all, dst_chunks).then_inc(s_da, 16)
            sp.wait_ge(s_zero, 1)
            sp.dma_start(X[:, 0:(B - 1) * D].rearrange("p (b d) -> p b d", d=D),
                         x[0:(B - 1) * P, :].rearrange("(b p) d -> p b d", p=P)).then_inc(s_in, 16)
            sp.dma_start(X[0:LAST, (B - 1) * D:B * D], x[(B - 1) * P:N, :]).then_inc(s_in, 16)
            for n, w in enumerate((w0, w1[0:D, :], w1[D:2 * D, :], w2, w3)):
                for o in (0, D):
                    sp.dma_start(Wd[o:o + D, n, o:o + D], w).then_inc(s_w, 16)
            with nc.allow_non_contiguous_dma(reason="columns of 64 values"):
                for n, v in enumerate((b1, b2, b3, g1, g2, g3, bt1, bt2, bt3)):
                    for o in (0, D):
                        sp.dma_start(vecs[o:o + D, n:n + 1], v.rearrange("(d o) -> d o", o=1)).then_inc(s_w, 16)
                sp.dma_start(gcol[:, :], gattr[0:1, :].rearrange("o d -> d o")).then_inc(s_w, 16)
            for o in (0, D):
                sp.dma_start(w1c[:, o:o + D], w1[2 * D:3 * D, :]).then_inc(s_w, 16)
            sp.dma_start(brow[:, :], b0.rearrange("(o d) -> o d", o=1).broadcast_to([P, D])).then_inc(s_w, 16)

            def load_edges(c, q):
                rows = ds(c * P, P)
                sp.dma_start(src_i[:, q, :], src_v[rows, :]).then_inc(s_ldA[q], 16)
                sp.dma_start(ea_s[:, q, :], ea_v[rows, :]).then_inc(s_ldA[q], 16)

            def load_dst(c, q):
                rows = ds(c * P, P)
                sp.dma_start(dst_i[:, q, :], dst_v[rows, :]).then_inc(s_ldB[q], 16)
                sp.dma_start(ew_s[:, q, :], ew_v[rows, :]).then_inc(s_ldB[q], 16)

            sp.wait_ge(s_nw, 1)
            load_edges(0, 0)
            load_dst(0, 0)
            load_edges(1, 1)
            sp.wait_ge(s_sp, 1)
            sp.dma_start(span_d, span_i[0:C, :]).then_inc(s_spo, 16)
            sp.dma_start(base_d, base_f[0:C, :]).then_inc(s_spo, 16)
            sp.wait_ge(s_spo, 32)
            sp.dma_start(spans[:, :], span_d.rearrange("(o c) f -> o (c f)", o=1)).then_inc(s_spl, 16)
            with nc.allow_non_contiguous_dma(reason="one row for all partitions"):
                sp.dma_start(bases[:, :], base_d.rearrange("(o c) f -> o (c f)", o=1).broadcast_to([P, C])).then_inc(s_spl, 16)
            for i in range(NG):
                sp.wait_ge(s_Hs, i + 2)
                sp.dma_start(h_tab[:, i * GC:(i + 1) * GC], hrow[:, i % 2, :]).then_inc(s_Ho[i % 2], 16)

            def load_next(c, q):
                sp.wait_ge(s_sidx, c - 1)
                load_edges(c, q)
                sp.wait_ge(s_win, c)
                load_dst(c - 1, 1 - q)

            with sp.Fori(0, (C - 3) // 2) as i:
                load_next(2 * i + 2, 0)
                load_next(2 * i + 3, 1)
            load_next(C - 1, 0)
            sp.wait_ge(s_win, C)
            load_dst(C - 1, 0)

            for k in range(K):
                sp.wait_ge(s_tab[k], 16 * G * C)
            tabs = sum_tab.rearrange("(k r) d -> k (r d)", k=K)[:, 0:NPAD * D].rearrange("k (p b d) -> p k (b d)", p=P, b=B)

            def load_tables(i, q):
                for k in range(K):
                    sp.dma_start(tg[:, q, k, :], tabs[:, k, ds(i * GC, GC)]).then_inc(s_tg[q], 16)

            sp.wait_ge(s_win, C + 2)
            load_tables(0, 0)
            load_tables(1, 1)
            with sp.Fori(0, (NG - 3) // 2) as i:
                sp.wait_ge(s_v, 2 * i + 1)
                load_tables(2 * i + 2, 0)
                sp.wait_ge(s_v, 2 * i + 2)
                load_tables(2 * i + 3, 1)
            sp.wait_ge(s_v, NG - 2)
            load_tables(NG - 1, 0)
            o_v = out[0:(B - 1) * P, :].rearrange("(b p) d -> p b d", p=P)
            for i in range(NG):
                sp.wait_ge(s_o, i + 1)
                rows = tg[:, i % 2, 0, :].rearrange("p (b d) -> p b d", d=D)
                nb = GB if i < NG - 1 else GB - 1
                sp.dma_start(o_v[:, i * GB:i * GB + nb, :], rows[:, 0:nb, :]).then_inc(s_out[i % 2], 16)
            sp.dma_start(out[(B - 1) * P:N, :], tg[0:LAST, (NG - 1) % 2, 0, GC - D:GC]).then_inc(s_out[(NG - 1) % 2], 16)
            sp.wait_ge(s_out[0], 16 * 5)
            sp.wait_ge(s_out[1], 16 * 3)

        @block.gpsimd
        def _(pool):
            nc.gpsimd.iota(iota_i[:, :], pattern=[[1, P]], base=0, channel_multiplier=0)
            nc.gpsimd.iota(pid_i[:, :], pattern=[[0, 1]], base=0, channel_multiplier=1)
            nc.gpsimd.iota(pw_i[:, :], pattern=[[0, 1]], base=190, channel_multiplier=-1)
            nc.gpsimd.iota(sel_i, pattern=[[1, T], [0, P]], base=0, channel_multiplier=0).then_inc(s_iota, 1)
            pool.wait_ge(s_zero, 1)
            for k in range(K):
                pool.dma_start(sum_tab[k * R:(k + 1) * R, :].rearrange("(p b) d -> p (b d)", p=P),
                               acc[:, :]).then_inc(s_tabz, 16)
            pool.wait_ge(s_tabz, 16 * K)

            def scatter(c, q, first=False):
                pool.wait_ge(s_sidx, c + 1)
                pool.wait_ge(s_Us, G * (c + 1) + 2)
                for t in range(T):
                    k, g = t % K, t // K
                    if not (first and g == 0):
                        pool.wait_ge(s_tab[k], 16 * (G * c + g))
                        pool.sem_inc(s_pace, 1)
                    pool.indirect_dma_start(
                        out=sum_tab, out_offset=bass.IndirectOffsetOnAxis(ap=sidx[:, q, t:t + 1], axis=0),
                        in_=ust[:, q, t * D:(t + 1) * D], in_offset=None,
                        element_offset=k * R * D, compute_op=ALU.add).then_inc(s_tab[k], 16)
                    if t == K - 1 and not first:
                        pool.sem_inc(s_free, 1)

            def gather(c, q):
                pool.wait_ge(s_gidx, c + 1)
                pool.wait_ge(s_win, c + 1)
                pool.sem_inc(s_pace, 1)
                for t in range(T):
                    pool.indirect_dma_start(
                        out=gat[:, q, t * D:(t + 1) * D], out_offset=None, in_=h_rows,
                        in_offset=bass.IndirectOffsetOnAxis(ap=gidx[:, q, t:t + 1], axis=0)).then_inc(s_g[q], 16)

            scatter(0, 0, first=True)
            pool.wait_ge(s_Ho[0], 16 * 4)
            pool.wait_ge(s_Ho[1], 16 * 3)
            gather(0, 0)
            with pool.Fori(0, (C - 1) // 2) as i:
                gather(2 * i + 1, 1)
                scatter(2 * i + 1, 1)
                gather(2 * i + 2, 0)
                scatter(2 * i + 2, 0)

        @block.scalar
        def _(act):
            act.wait_ge(s_const, 1)

            def square(n, q):
                act.wait_ge(s_xc, n + 1)
                nc.scalar.activation(sq[:, q, :], xc[:, q, :], ACT.Square).then_inc(s_sq, 1)

            def deviation(n, q):
                act.wait_ge(s_var, n + 1)
                nc.scalar.activation(ln_r[:, q, :], ln_v[:, q, :], ACT.Sqrt, bias=eps_t[:, :], scale=1.0 / D).then_inc(s_std, 1)

            def transposed_h(n):
                act.wait_ge(s_hTp, n + 1)
                nc.scalar.copy(hT[:, 0, :], T_all).then_inc(s_hTs, 1)

            def table_step(i, q):
                square(i + 1, 1 - q)
                deviation(i, q)
                transposed_h(i)

            square(0, 0)
            with act.Fori(0, (NG - 1) // 2) as i:
                table_step(2 * i, 0)
                table_step(2 * i + 1, 1)
            deviation(NG - 1, 0)
            transposed_h(NG - 1)

            def round_messages(c, q):
                for k in range(3):
                    act.wait_ge(s_md, 3 * c + k + 1)
                    nc.scalar.copy(msg_p[:, :, k, :], gat[:, q, :].rearrange("p (t d) -> p t d", d=D)).then_inc(s_mr, 1)

            def stage(c, q, loads):
                act.wait_ge(s_ldA[q], loads)
                for k in range(3):
                    if k:
                        act.wait_ge(s_ed, 2 * c + k)
                    nc.scalar.copy(ea_p[:, k, :], ea_s[:, q, :]).then_inc(s_er, 1)
                act.wait_ge(s_free, c + 1)
                for g in range(G):
                    b = (q + g) % 2
                    act.wait_ge(s_U, G * c + g + 3)
                    nc.scalar.copy(ust[:, q, g * GT * D:(g + 1) * GT * D], u_ps[b])
                    nc.scalar.copy(pw_s[:, g * GT:(g + 1) * GT], pw_ps[b]).then_inc(s_Us, 1)

            stage(0, 0, 32)
            stage(1, 1, 32)
            with act.Fori(0, (C - 3) // 2) as i:
                round_messages(2 * i, 0)
                stage(2 * i + 2, 0, 32 * i + 64)
                round_messages(2 * i + 1, 1)
                stage(2 * i + 3, 1, 32 * i + 64)
            round_messages(C - 3, 0)
            stage(C - 1, 0, 32 * ((C + 1) // 2))
            round_messages(C - 2, 1)
            round_messages(C - 1, 0)

            act.wait_ge(s_b1, 1)

            def first_layer(i):
                transposed_h(i + NG)
                act.wait_ge(s_vTp, i + 2)
                nc.scalar.copy(hT[:, 1, :], V_all).then_inc(s_vTs, 1)
                for h in range(2):
                    act.wait_ge(s_z, 2 * i + h + 1)
                    nc.scalar.activation(Rl[:, ds(i * GC + h * HALF, HALF)], Z_ps[h], ACT.Relu,
                                         bias=bias[:, 0:1]).then_inc(s_r, 1)

            square(NG, 0)
            with act.Fori(0, (NG - 1) // 2) as i:
                for q in range(2):
                    square(2 * i + q + NG + 1, 1 - q)
                    deviation(2 * i + q + NG, q)
                    first_layer(2 * i + q)
            deviation(2 * NG - 1, 0)
            first_layer(NG - 1)
            for n in range(3):
                if n:
                    act.wait_ge(s_wr, n)
                    with act.Fori(0, NG) as i:
                        for h in range(2):
                            act.wait_ge(s_z, 2 * NG * n + 2 * i + h + 1)
                            nc.scalar.activation(Rl[:, ds(i * GC + h * HALF, HALF)], Z_ps[h], ACT.Relu,
                                                 bias=bias[:, n:n + 1]).then_inc(s_r, 1)
                act.wait_ge(s_mean, n + 1)
                nc.scalar.activation(acc[:, 0:COLS - BAD], Rl[:, 0:COLS - BAD], ACT.Square, bias=st[:, 2:3],
                                     accum_out=st[:, 3:4])
                nc.scalar.activation(acc[0:D, COLS - BAD:COLS], Rl[0:D, COLS - BAD:COLS], ACT.Square,
                                     bias=st[0:D, 2:3], accum_out=st[0:D, 4:5]).then_inc(s_dev, 1)
                act.wait_ge(s_vs, n + 1)
                nc.scalar.activation(st[:, 7:8], st[:, 6:7], ACT.Sqrt, bias=eps_t[:, :], scale=1.0 / N).then_inc(s_sd, 1)

        @block.vector
        def _(dve):
            V = nc.vector

            def fence():
                V.drain()

            def by_block(a):
                return a.rearrange("p (b d) -> p b d", d=D)

            V.memset(acc[:, :], 0.0)
            V.memset(X[:, (B - 1) * D:B * D], 0.0)
            V.memset(Wd[:, :, :], 0.0)
            V.memset(cnt[:, :], 0.0)
            V.memset(st[:, :], 0.0)
            V.memset(parts[:, :], 0.0)
            V.memset(eps_t[:, :], EPS)
            V.drain().then_inc(s_zero, 1)
            dve.wait_ge(s_iota, 1)
            V.tensor_copy(iota_f[:, :], iota_i[:, :])
            V.tensor_copy(iota_b[:, :], iota_i[:, :])
            V.tensor_copy(pid_f[:, :], pid_i[:, :])
            V.tensor_single_scalar(mod_i[:, :], iota_i[:, :], D - 1, ALU.bitwise_and)
            V.tensor_single_scalar(pmod_i[:, :], pid_i[:, :], D - 1, ALU.bitwise_and)
            V.tensor_single_scalar(pw_b[:, :], pw_i[:, :], 23, ALU.logical_shift_left)
            fence()
            V.tensor_copy(mod_f[:, :], mod_i[:, :])
            V.tensor_copy(pmod_f[:, :], pmod_i[:, :])
            V.tensor_scalar(kmod[:, :], pid_f[:, :], float(T), -float(T), ALU.is_ge, ALU.mult)
            V.tensor_scalar(spare_row[:, :], pid_f[:, :], float(NPAD), None, ALU.add)
            V.tensor_scalar(thr[:, :], pw_f, 2.5, None, ALU.mult)
            V.tensor_copy(pw_h[:, :], pw_f)
            V.tensor_scalar(ident[:, :], iota_f[:, :], pid_f[:, :], None, ALU.is_equal)
            V.tensor_scalar(ident_b[:, :], iota_f[:, :], pid_f[:, :], None, ALU.is_equal)
            V.tensor_scalar(before[:, :], iota_f[:, :], pid_f[:, :], None, ALU.is_gt)
            fence()
            V.tensor_tensor(kmod[:, :], kmod[:, :], pid_f[:, :], ALU.add)
            V.tensor_scalar(fold[:, :], mod_f[:, :], pmod_f[:, :], None, ALU.is_equal)
            fence()
            V.tensor_scalar(sel[:, :], sel_i, kmod[0:2 * T, :], None, ALU.is_equal)
            V.drain().then_inc(s_const, 1)
            V.drain().then_inc(s_U, 2)
            V.drain().then_inc(s_Us, 2)
            V.drain().then_inc(s_M, 2)
            V.drain().then_inc(s_cm, 2)
            V.drain().then_inc(s_cu, 1)
            V.drain().then_inc(s_free, 2)
            V.drain().then_inc(s_Sm, G)
            V.drain().then_inc(s_acc, 1)
            V.drain().then_inc(s_win, 2)
            V.drain().then_inc(s_Hs, 1)
            V.drain().then_inc(s_vTp, 1)

            dve.wait_ge(s_da, 16)
            V.tensor_reduce(mm_i[0:C, 0:1], dst_all, AX.X, ALU.min)
            V.tensor_reduce(mm_i[0:C, 1:2], dst_all, AX.X, ALU.max)
            fence()
            V.tensor_single_scalar(mm_s[0:C, :], mm_i[0:C, :], 7, ALU.arith_shift_right)
            V.memset(span_f[0:C, 3:4], 0.0)
            fence()
            V.tensor_copy(span_f[0:C, 0:1], mm_s[0:C, 0:1])
            V.tensor_copy(mm_f[0:C, :], mm_s[0:C, 1:2])
            fence()
            V.scalar_tensor_tensor(out=span_f[0:C, 1:2], in0=mm_f[0:C, :], scalar=1.0, in1=span_f[0:C, 0:1],
                                   op0=ALU.add, op1=ALU.subtract)
            V.tensor_scalar(base_f[0:C, :], span_f[0:C, 0:1], float(P), None, ALU.mult)
            V.drain().then_inc(s_nw, 1)
            dve.wait_ge(s_w, 16 * 32)
            dve.wait_ge(s_cum, 1)
            V.tensor_copy(span_f[0:C, 2:3], small_ps[0:C, 0:1])
            V.tensor_tensor(bias[:, 0:1], small_ps[:, 1:2], vecs[:, 0:1], ALU.add).then_inc(s_b1, 1)
            fence()
            V.tensor_copy(span_i[0:C, :], span_f[0:C, :]).then_inc(s_sp, 1)

            def centre(i, q, second=False):
                xg = X[:, ds(i * GC, GC)]
                if second:
                    V.tensor_tensor(xg, xg, acc[:, ds(i * GC, GC)], ALU.add)
                    fence()
                V.tensor_reduce(ln_s[:, :], by_block(xg), AX.X, ALU.add)
                fence()
                V.tensor_scalar(ln_m[:, :], ln_s[:, :], 1.0 / D, None, ALU.mult)
                fence()
                V.tensor_tensor(by_block(xc[:, q, :]), by_block(xg), ln_m[:, :].unsqueeze(2).broadcast_to([P, GB, D]),
                                ALU.subtract).then_inc(s_xc, 1)

            def normalise(n, q):
                dve.wait_ge(s_sq, n + 1)
                V.tensor_reduce(ln_v[:, q, :], by_block(sq[:, q, :]), AX.X, ALU.add).then_inc(s_var, 1)
                dve.wait_ge(s_std, n + 1)
                V.reciprocal(ln_q[:, :], ln_r[:, q, :])
                fence()
                V.scalar_tensor_tensor(out=by_block(hg[:, q, :]), in0=by_block(xc[:, q, :]), scalar=0.0,
                                       in1=ln_q[:, :].unsqueeze(2).broadcast_to([P, GB, D]),
                                       op0=ALU.max, op1=ALU.mult).then_inc(s_h, 1)

            def table_rows(i):
                dve.wait_ge(s_Hp, i + 1)
                if i >= 2:
                    dve.wait_ge(s_Ho[i % 2], 16 * (i // 2))
                V.tensor_tensor(by_block(hrow[:, i % 2, :]), by_block(V_all),
                                brow[:, :].unsqueeze(1).broadcast_to([P, GB, D]), ALU.add).then_inc(s_Hs, 1)

            dve.wait_ge(s_in, 32)
            centre(0, 0)
            for i in range(NG):
                if i + 1 < NG:
                    centre(i + 1, (i + 1) % 2)
                normalise(i, i % 2)
                if i:
                    table_rows(i - 1)
            table_rows(NG - 1)

            def prepare(c, q, loads):
                dve.wait_ge(s_ldA[q], loads)
                V.tensor_single_scalar(hi_i[:, :], src_i[:, q, :], 7, ALU.arith_shift_right)
                V.tensor_single_scalar(lo_i[:, :], src_i[:, q, :], P - 1, ALU.bitwise_and)
                fence()
                V.tensor_copy(hi_f[:, :], hi_i[:, :])
                V.tensor_copy(lo_f[:, :], lo_i[:, :])
                fence()
                V.tensor_scalar(parts[:, 0:T], hi_f[:, :], float(P), None, ALU.mult)
                V.tensor_copy(parts[:, T:2 * T], lo_f[:, :])
                V.scalar_tensor_tensor(out=src_f[:, :], in0=hi_f[:, :], scalar=float(P), in1=lo_f[:, :],
                                       op0=ALU.mult, op1=ALU.add)
                V.scalar_tensor_tensor(out=row_f[:, :], in0=lo_f[:, :], scalar=float(B), in1=hi_f[:, :],
                                       op0=ALU.mult, op1=ALU.add)
                V.drain().then_inc(s_parts, 1)
                V.tensor_copy(gidx[:, q, :], row_f[:, :]).then_inc(s_gidx, 1)
                for k in range(2):
                    dve.wait_ge(s_er, 3 * c + k + 1)
                    V.tensor_tensor(ea_s[:, q, :], ea_s[:, q, :], ea_p[:, k, :], ALU.subtract).then_inc(s_ed, 1)
                dve.wait_ge(s_pT, c + 1)
                V.tensor_copy(partsT[:, :], ptT_ps[0:2 * T, :]).then_inc(s_pTs, 1)
                for g in range(G):
                    b = (q + g) % 2
                    n = G * c + g
                    dve.wait_ge(s_cm, n + 1)
                    tiles = slice(g * GT, (g + 1) * GT)
                    V.tensor_tensor(oh_lo[:, b, :].rearrange("p (t i) -> p t i", i=P),
                                    iota_b[:, :].unsqueeze(1).broadcast_to([P, GT, P]),
                                    lo_f[:, tiles].unsqueeze(2).broadcast_to([P, GT, P]), ALU.is_equal)
                    V.tensor_tensor(oh_hi[:, b, :].rearrange("p (t i) -> p t i", i=B),
                                    iota_b[:, 0:B].unsqueeze(1).broadcast_to([P, GT, B]),
                                    hi_f[:, tiles].unsqueeze(2).broadcast_to([P, GT, B]), ALU.is_equal).then_inc(s_oh, 1)
                    dve.wait_ge(s_bc, n + 1)
                    dve.wait_ge(s_U, n + 1)
                    V.tensor_tensor(Mt[:, b, :].rearrange("p (t i) -> p t i", i=P),
                                    bc_ps[b].rearrange("p (t i) -> p t i", i=P),
                                    src_f[:, g * GT:(g + 1) * GT].unsqueeze(2).broadcast_to([P, GT, P]),
                                    ALU.is_equal).then_inc(s_M, 1)
                dve.wait_ge(s_cm, G * (c + 1) + 2)
                V.tensor_tensor(cnt[:, :], cnt[:, :], cnt_ps, ALU.add).then_inc(s_cu, 1)
                dve.wait_ge(s_Us, G * (c + 1) + 2)
                V.tensor_scalar(flag[:, :], pw_s[:, :], thr[:, :], None, ALU.is_lt)
                V.tensor_scalar(row_f[:, :], row_f[:, :], spare_row[:, :], None, ALU.subtract)
                fence()
                V.tensor_tensor(row_f[:, :], row_f[:, :], flag[:, :], ALU.mult)
                fence()
                dve.wait_ge(s_free, c + 1)
                V.tensor_scalar(sidx[:, q, :], row_f[:, :], spare_row[:, :], None, ALU.add).then_inc(s_sidx, 1)

            def windows(c, q, pairs):
                dve.wait_ge(s_ldB[q], 32 * pairs)
                dve.wait_ge(s_g[q], 16 * T * pairs)
                rows = gat[:, q, :].rearrange("p (t d) -> p t d", d=D)
                V.tensor_tensor(rows, rows, ew_s[:, q, :].unsqueeze(2).broadcast_to([P, T, D]), ALU.mult).then_inc(s_md, 1)
                V.tensor_copy(drel[:, :], dst_i[:, q, :])
                fence()
                V.tensor_scalar(drel[:, :], drel[:, :], bases[:, ds(c, 1)], None, ALU.subtract)
                fence()
                for k in range(2):
                    dve.wait_ge(s_mr, 3 * c + k + 1)
                    V.tensor_tensor(rows, rows, msg_p[:, :, k, :], ALU.subtract).then_inc(s_md, 1)
                first = dve.value_load(spans[0:1, ds(4 * c, 1)], min_val=0, max_val=B - 1)
                count = dve.value_load(spans[0:1, ds(4 * c + 1, 1)], min_val=1, max_val=B)
                done = dve.value_load(spans[0:1, ds(4 * c + 2, 1)], min_val=0, max_val=B * C)
                with dve.Fori(0, count) as j:
                    for g in range(G):
                        dve.wait_ge(s_Sm, (done + j) * G + g + 1)
                        V.tensor_tensor(St[:, g, :].rearrange("p (t i) -> p t i", i=P),
                                        iota_b[:, :].unsqueeze(1).broadcast_to([P, GT, P]),
                                        drel[:, g * GT:(g + 1) * GT].unsqueeze(2).broadcast_to([P, GT, P]),
                                        ALU.is_equal).then_inc(s_S, 1)
                    dve.wait_ge(s_Sm, (done + j) * G + 2 * G)
                    V.tensor_scalar(drel[:, :], drel[:, :], float(P), None, ALU.subtract)
                    a = acc[:, ds(nc.s_assert_within(first + j, min_val=0, max_val=B - 1) * D, D)]
                    V.tensor_reduce(wsum[:, :], win_ps.rearrange("p (k d) -> p d k", k=3), AX.X, ALU.add).then_inc(s_acc, 1)
                    fence()
                    V.tensor_tensor(a, a, wsum[:, :], ALU.add)
                    fence()
                V.drain().then_inc(s_win, 1)

            dve.wait_ge(s_spl, 32)
            prepare(0, 0, 32)
            prepare(1, 1, 32)
            with dve.Fori(0, (C - 3) // 2) as i:
                windows(2 * i, 0, i + 1)
                prepare(2 * i + 2, 0, 32 * i + 64)
                windows(2 * i + 1, 1, i + 1)
                prepare(2 * i + 3, 1, 32 * i + 64)
            windows(C - 3, 0, (C - 1) // 2)
            prepare(C - 1, 0, 32 * ((C + 1) // 2))
            windows(C - 2, 1, (C - 1) // 2)
            windows(C - 1, 0, (C + 1) // 2)

            V.tensor_scalar(rc[:, :], cnt[:, :], 1.0, None, ALU.max)
            fence()
            V.reciprocal(rc[:, :], rc[:, :])

            def mean_edges(i, q, loads):
                dve.wait_ge(s_tg[q], 16 * K * loads)
                V.tensor_tensor(tsum[:, :], tg[:, q, 0, :], tg[:, q, 1, :], ALU.add)
                for k in range(2, K):
                    fence()
                    V.tensor_tensor(tsum[:, :], tsum[:, :], tg[:, q, k, :], ALU.add)
                fence()
                dve.wait_ge(s_vTp, i + 1)
                V.tensor_tensor(by_block(ve[:, :]), by_block(tsum[:, :]),
                                rc[:, ds(i * GB, GB)].unsqueeze(2).broadcast_to([P, GB, D]), ALU.mult).then_inc(s_v, 1)

            fence()
            centre(0, 0, second=True)
            with dve.Fori(0, (NG - 1) // 2) as i:
                for q in range(2):
                    n = 2 * i + q
                    centre(n + 1, 1 - q, second=True)
                    dve.wait_ge(s_hTp, NG + n - 1)
                    normalise(NG + n, q)
                    mean_edges(n, q, i + 1)
            normalise(2 * NG - 1, 0)
            mean_edges(NG - 1, 0, (NG + 1) // 2)

            for n in range(3):
                dve.wait_ge(s_r, 2 * NG * (n + 1))
                V.memset(Rl[D:P, COLS - BAD:COLS], 0.0)
                fence()
                V.tensor_reduce(st[:, 0:1], Rl[:, :], AX.X, ALU.add).then_inc(s_sum, 1)
                dve.wait_ge(s_tot, n + 1)
                V.tensor_scalar(st[:, 1:2], small_ps[:, 2:3], 1.0 / N, None, ALU.mult)
                V.tensor_scalar(st[:, 2:3], small_ps[:, 2:3], -1.0 / N, None, ALU.mult).then_inc(s_mean, 1)
                dve.wait_ge(s_dev, n + 1)
                V.tensor_tensor(st[:, 5:6], st[:, 3:4], st[:, 4:5], ALU.add).then_inc(s_vp, 1)
                dve.wait_ge(s_vt, n + 1)
                V.tensor_copy(st[:, 6:7], small_ps[:, 3:4]).then_inc(s_vs, 1)
                dve.wait_ge(s_sd, n + 1)
                V.reciprocal(st[:, 8:9], st[:, 7:8])
                fence()
                V.tensor_tensor(st[:, 9:10], st[:, 8:9], vecs[:, 3 + n:4 + n], ALU.mult)
                fence()
                V.tensor_tensor(st[:, 10:11], st[:, 9:10], st[:, 1:2], ALU.mult)
                fence()
                V.tensor_tensor(st[:, 11:12], vecs[:, 6 + n:7 + n], st[:, 10:11], ALU.subtract).then_inc(s_bn, 1)
                if n < 2:
                    V.tensor_scalar(Ws[:, :], Wd[:, 3 + n, :], st[:, 9:10], None, ALU.mult)
                    dve.wait_ge(s_bp, n + 1)
                    V.tensor_tensor(bias[:, n + 1:n + 2], small_ps[:, 4:5], vecs[:, n + 1:n + 2], ALU.add).then_inc(s_wr, 1)
            fence()
            for i in range(NG):
                V.tensor_scalar(hg[:, i % 2, :], Rl[:, i * GC:(i + 1) * GC], st[:, 9:10], st[:, 11:12],
                                ALU.mult, ALU.add).then_inc(s_y, 1)
                dve.wait_ge(s_yT, i + 1)
                if i >= 2:
                    dve.wait_ge(s_out[i % 2], 16 * (i // 2))
                V.tensor_tensor(tg[:, i % 2, 0, :], X[:, i * GC:(i + 1) * GC], T_all, ALU.add).then_inc(s_o, 1)

        @block.tensor
        def _(pe):
            mm = nc.tensor.matmul

            pe.wait_ge(s_const, 1)
            pe.wait_ge(s_nw, 1)
            pe.wait_ge(s_w, 16 * 32)
            mm(small_ps[0:C, 0:1], before[0:C, 0:C], span_f[0:C, 1:2], start=True, stop=True)
            mm(small_ps[:, 1:2], w1c[:, :], gcol[:, :], start=True, stop=True).then_inc(s_cum, 1)

            def transpose_h(q):
                for j in range(GP):
                    last = nc.tensor.transpose(T_ps[j], hg[:, q, j * P:(j + 1) * P], ident[:, :])
                return last

            def table_product(i, q):
                pe.wait_ge(s_h, i + 1)
                transpose_h(q).then_inc(s_hTp, 1)
                pe.wait_ge(s_hTs, i + 1)
                pe.wait_ge(s_Hs, i + 1)
                for j in range(GP):
                    last = mm(V_ps[j], hT[:, 0, j * P:(j + 1) * P], Wd[:, 0, :], start=True, stop=True)
                last.then_inc(s_Hp, 1)

            with pe.Fori(0, (NG - 1) // 2) as i:
                table_product(2 * i, 0)
                table_product(2 * i + 1, 1)
            table_product(NG - 1, 0)

            def broadcast(c, q, g):
                b = (q + g) % 2
                pe.wait_ge(s_M, G * c + g + 1)
                for j in range(GT):
                    t = g * GT + j
                    last = mm(bc_ps[b][:, j * P:(j + 1) * P], sel[:, t * P:(t + 1) * P], partsT[:, :], start=True, stop=True)
                last.then_inc(s_bc, 1)

            def prepare(c, q):
                pe.wait_ge(s_parts, c + 1)
                pe.wait_ge(s_cu, c + 1)
                nc.tensor.transpose(ptT_ps, parts[:, :], ident_b[:, :]).then_inc(s_pT, 1)
                pe.wait_ge(s_pTs, c + 1)
                broadcast(c, q, 0)
                broadcast(c, q, 1)
                for g in range(G):
                    b = (q + g) % 2
                    n = G * c + g
                    pe.wait_ge(s_M, n + 3)
                    pe.wait_ge(s_Us, n + 1)
                    if g == 0:
                        pe.wait_ge(s_er, 3 * c + 3)
                    for j in range(GT):
                        t = g * GT + j
                        mask = Mt[:, b, j * P:(j + 1) * P]
                        for k in range(3):
                            mm(u_ps[b][:, j * D:(j + 1) * D], mask, ea_p[:, k, t * D:(t + 1) * D], start=(k == 0), stop=(k == 2))
                        last = mm(pw_ps[b][:, j:j + 1], mask, pw_h[:, :], start=True, stop=True)
                    last.then_inc(s_U, 1)
                    pe.wait_ge(s_oh, n + 1)
                    for j in range(GT):
                        t = g * GT + j
                        last = mm(cnt_ps, oh_lo[:, b, j * P:(j + 1) * P], oh_hi[:, b, j * B:(j + 1) * B],
                                  start=(t == 0), stop=(t == T - 1))
                    last.then_inc(s_cm, 1)
                    if g + 2 < G:
                        broadcast(c, q, g + 2)

            def windows(c, q):
                pe.wait_ge(s_mr, 3 * c + 3)
                count = pe.value_load(spans[0:1, ds(4 * c + 1, 1)], min_val=1, max_val=B)
                done = pe.value_load(spans[0:1, ds(4 * c + 2, 1)], min_val=0, max_val=B * C)
                with pe.Fori(0, count) as j:
                    pe.wait_ge(s_acc, done + j + 1)
                    for g in range(G):
                        pe.wait_ge(s_S, (done + j) * G + g + 1)
                        for t in range(GT):
                            e = g * GT + t
                            last = mm(win_ps, St[:, g, t * P:(t + 1) * P], msg_p[:, e, :, :],
                                      start=(e == 0), stop=(e == T - 1))
                        last.then_inc(s_Sm, 1)

            pe.wait_ge(s_spl, 32)
            prepare(0, 0)
            prepare(1, 1)
            with pe.Fori(0, (C - 3) // 2) as i:
                windows(2 * i, 0)
                prepare(2 * i + 2, 0)
                windows(2 * i + 1, 1)
                prepare(2 * i + 3, 1)
            windows(C - 3, 0)
            prepare(C - 1, 0)
            windows(C - 2, 1)
            windows(C - 1, 0)

            def first_layer(i, q):
                pe.wait_ge(s_h, NG + i + 1)
                transpose_h(q).then_inc(s_hTp, 1)
                pe.wait_ge(s_v, i + 1)
                for j in range(GP):
                    last = nc.tensor.transpose(V_ps[j], ve[:, j * P:(j + 1) * P], ident[:, :])
                last.then_inc(s_vTp, 1)
                pe.wait_ge(s_hTs, NG + i + 1)
                pe.wait_ge(s_vTs, i + 1)
                for h in range(2):
                    cols = slice(h * HALF, (h + 1) * HALF)
                    mm(Z_ps[h], Wd[:, 1, :], hT[:, 0, cols], start=True, stop=False)
                    mm(Z_ps[h], Wd[:, 2, :], hT[:, 1, cols], start=False, stop=True).then_inc(s_z, 1)

            with pe.Fori(0, (NG - 1) // 2) as i:
                first_layer(2 * i, 0)
                first_layer(2 * i + 1, 1)
            first_layer(NG - 1, 0)
            for n in range(3):
                if n:
                    pe.wait_ge(s_wr, n)
                    with pe.Fori(0, NG) as i:
                        for h in range(2):
                            pe.wait_ge(s_r, 2 * NG * n + 2 * i + h - 1)
                            mm(Z_ps[h], Ws[:, :], Rl[:, ds(i * GC + h * HALF, HALF)], start=True, stop=True).then_inc(s_z, 1)
                pe.wait_ge(s_sum, n + 1)
                mm(small_ps[:, 2:3], fold[:, :], st[:, 0:1], start=True, stop=True).then_inc(s_tot, 1)
                pe.wait_ge(s_vp, n + 1)
                mm(small_ps[:, 3:4], fold[:, :], st[:, 5:6], start=True, stop=True).then_inc(s_vt, 1)
                if n < 2:
                    pe.wait_ge(s_bn, n + 1)
                    mm(small_ps[:, 4:5], Wd[:, 3 + n, :], st[:, 11:12], start=True, stop=True).then_inc(s_bp, 1)
            for i in range(NG):
                pe.wait_ge(s_y, i + 1)
                transpose_h(i % 2).then_inc(s_yT, 1)


_INS = ["x", "src", "dst", "edge_attr_64", "edge_weight", "L0_gnn_W", "L0_gnn_b", "L1_gnn_global_attr",
        "L1_gnn_W1", "L1_gnn_b1", "L1_gnn_W2", "L1_gnn_b2", "L1_gnn_W3", "L1_gnn_b3",
        "L1_gnn_g1", "L1_gnn_bt1", "L1_gnn_g2", "L1_gnn_bt2", "L1_gnn_g3", "L1_gnn_bt3"]


def kernel(**inputs):
    import numpy as np
    import concourse.bacc as bacc
    from concourse.bass_utils import run_bass_kernel_spmd

    nc = bacc.Bacc("TRN2", target_bir_lowering=False, num_devices=1)
    arrays, args = {}, []
    for name in _INS:
        a = np.ascontiguousarray(inputs[name])
        arrays[f"in_{name}"] = a
        args.append(nc.dram_tensor(f"in_{name}", a.shape, mybir.dt.from_np(a.dtype), kind="ExternalInput").ap())
    out = nc.dram_tensor("out_0", (N, D), mybir.dt.float32, kind="ExternalOutput").ap()
    gnn_kernel(nc, *args, out)
    r = run_bass_kernel_spmd(nc, [arrays], core_ids=[0])
    return r.results[0]["out_0"]
```

```python
import concourse.bass as bass
from concourse import mybir
from contextlib import ExitStack

N = 12500
E = 400000
D = 64
P = 128
B = -(-N // P)
LAST = N - (B - 1) * P
NPAD = B * P
T = 25
CH = P * T
C = E // CH
G = 5
GT = T // G
TG = 16
GG = 4
GTG = TG // GG
EG = C * P * TG
TA = 18
NT = (E - EG) // P
NB = -(-NT // TA)
TL = NT - (NB - 1) * TA
SPAN = 7
TF = NT // C
W = D + 1
K = GT
R = NPAD + P
NG = 7
GB = B // NG
GC = GB * D
GP = GB // 2
COLS = B // 2 * P
BAD = P - LAST
HALF = GC // 2
KEY = SPAN * B
KH = KEY // 2
RA = TA * SPAN
OUTSIDE = 16384.0
EPS = 1e-5
assert C * CH == E and C % 2 == 1 and B % (2 * NG) == 0 and T % K == 0
assert NT * P == E - EG and TF * C == NT and 2 * TL == TA and RA <= P and NB == (C + 1) // 2


def gnn_kernel(nc, x, src, dst, ea, ew, w0, b0, gattr, w1, b1, w2, b2, w3, b3, g1, bt1, g2, bt2, g3, bt3, out):
    f32, bf16, i32 = mybir.dt.float32, mybir.dt.bfloat16, mybir.dt.int32
    ALU, ACT, AX = mybir.AluOpType, mybir.ActivationFunctionType, mybir.AxisListType
    ds = bass.ds

    src_v = src.rearrange("(c t) -> c t", t=T)
    dst_v = dst[0:EG].rearrange("(c t) -> c t", t=TG)
    gsrc_v = src[0:EG].rearrange("(c t) -> c t", t=TG)
    ew_v = ew[0:EG].rearrange("(c t) -> c t", t=TG)
    rest = [a[EG:E].rearrange("(t e) -> t e", e=P) for a in (src, dst, ew)]
    rest_f = [a[EG:E].rearrange("(c t) -> c t", t=TF) for a in (src, dst, ew)]
    ea_v = ea.rearrange("(c t) d -> c (t d)", t=T)
    dst_chunks = dst[0:EG].rearrange("(c e) -> c e", e=P * TG)
    dst_batches = dst[EG:EG + (NB - 1) * TA * P].rearrange("(b e) -> b e", e=TA * P)
    dst_last = dst[EG + (NB - 1) * TA * P:E].rearrange("(b e) -> b e", b=1)

    h_tab = nc.dram_tensor("h_tab", [P, B * D], f32).ap()
    h_rows = h_tab.rearrange("p (b d) -> (p b) d", d=D)
    sum_tab = nc.dram_tensor("sum_tab", [K * R, W], f32).ap()
    span_d = nc.dram_tensor("span_d", [C, 4], i32).ap()
    base_d = nc.dram_tensor("base_d", [C, 2], f32).ap()

    ctx = ExitStack()
    with ctx:
        def sb(name, shape, dt=f32):
            return ctx.enter_context(nc.sbuf_tensor(name, shape, dt))

        def sem(name):
            return ctx.enter_context(nc.semaphore(name))

        big = sb("big", [P, B * D + 10 * GC])
        X = big[:, 0:B * D]
        acc = sb("acc", [P, (B + 1) * W])
        Rl = sb("Rl", [P, COLS])
        rows_sb = sb("rows_sb", [P, 2 * K * GB * W])
        TD, TW, TGD = T * D, T * W, TG * D
        ea_s = rows_sb[:, 0:2 * TD].rearrange("p (q n) -> p q n", q=2)
        ust = rows_sb[:, 2 * TD:2 * TD + 2 * TW].rearrange("p (q n) -> p q n", q=2)
        gat = rows_sb[:, 2 * TD + 2 * TW:2 * TD + 2 * TW + 2 * TGD].rearrange("p (q n) -> p q n", q=2)
        tg = rows_sb[:, :].rearrange("p (q k n) -> p q k n", q=2, k=K)
        H = Rl
        src_i = sb("src_i", [P, 2, T], i32)
        dst_i = sb("dst_i", [P, 2, TG], i32)
        gsrc_i = sb("gsrc_i", [P, 2, TG], i32)
        ew_s = sb("ew_s", [P, 2, TG])
        gidx = sb("gidx", [P, 2, TG], i32)
        sidx = sb("sidx", [P, 2, T], i32)
        hi_i = sb("hi_i", [P, T], i32)
        lo_i = sb("lo_i", [P, T], i32)
        hi_f = sb("hi_f", [P, T])
        lo_f = sb("lo_f", [P, T])
        src_f = sb("src_f", [P, T])
        row_f = sb("row_f", [P, T])
        flag = sb("flag", [P, T])
        parts = sb("parts", [P, P], bf16)
        partsT = sb("partsT", [2 * T, P], bf16)
        pw_s = sb("pw_s", [P, T])
        Mt = sb("Mt", [P, 2, GT * P], bf16)
        drel = sb("drel", [P, TG])
        ghi_i = sb("ghi_i", [P, TG], i32)
        glo_i = sb("glo_i", [P, TG], i32)
        ghi_f = sb("ghi_f", [P, TG])
        glo_f = sb("glo_f", [P, TG])
        St = sb("St", [P, GG, GTG * P], bf16)
        ea_p = sb("ea_p", [P, 3, T, W], bf16)
        msg_p = sb("msg_p", [P, TG, 3, D], bf16)
        wsum = sb("wsum", [P, D])
        iota_i = sb("iota_i", [P, P], i32)
        iota_f = sb("iota_f", [P, P])
        iota_b = sb("iota_b", [P, P], bf16)
        mod_i = sb("mod_i", [P, P], i32)
        mod_f = sb("mod_f", [P, P])
        pid_i = sb("pid_i", [P, 1], i32)
        pid_f = sb("pid_f", [P, 1])
        pmod_i = sb("pmod_i", [P, 1], i32)
        pmod_f = sb("pmod_f", [P, 1])
        kmod = sb("kmod", [P, 1])
        spare_row = sb("spare_row", [P, 1])
        ident = sb("ident", [P, P])
        ident_b = sb("ident_b", [P, P], bf16)
        fold = sb("fold", [P, P])
        before = sb("before", [P, P])
        sel_i = rows_sb[0:2 * T, 2 * TD:2 * TD + T * P].bitcast(i32)
        sel = sb("sel", [2 * T, T * P], bf16)
        pw_i = sb("pw_i", [P, 1], i32)
        pw_b = sb("pw_b", [P, 1], i32)
        pw_h = sb("pw_h", [P, 1], bf16)
        pw_f = pw_b[:, :].bitcast(f32)
        thr = sb("thr", [P, 1])
        dst_all = rows_sb[0:C, 2 * TD + 2 * TW:2 * TD + 2 * TW + P * TG].bitcast(i32)
        mm_i = sb("mm_i", [P, 2], i32)
        mm_f = sb("mm_f", [P, 1])
        mm_s = sb("mm_s", [P, 2], i32)
        span_f = sb("span_f", [P, 4])
        span_i = sb("span_i", [P, 4], i32)
        base_f = sb("base_f", [P, 2])
        spans = sb("spans", [1, C * 4], i32)
        bases = sb("bases", [P, 2 * C])
        Wd = sb("Wd", [P, 5, P])
        w1c = sb("w1c", [D, P])
        gcol = sb("gcol", [D, 1])
        brow = sb("brow", [P, D])
        vecs = sb("vecs", [P, 9])
        Ws = sb("Ws", [P, P])
        node_sb = big[:, B * D:B * D + 10 * GC]
        pairs_sb = node_sb[:, 0:8 * GC].rearrange("p (k q n) -> p k q n", k=4, q=2)
        hg, xc, sq, hT = pairs_sb[:, 0], pairs_sb[:, 1], pairs_sb[:, 2], pairs_sb[:, 3]
        ve = node_sb[:, 9 * GC:10 * GC]
        A = big[:, 0:TA * KEY]
        A_rows = A.rearrange("p (r h) -> p r h", h=B)
        dst_rest = node_sb[0:NB, 10 * GC - TA * P:10 * GC].bitcast(i32)
        Sf = node_sb[:, 0:TF * P]
        arow_i = sb("arow_i", [TA, 3, P], i32)
        ahl_i = sb("ahl_i", [TA, 2, P], i32)
        arow = sb("arow", [TA, 3, P])
        abase_i = sb("abase_i", [TA, 1], i32)
        abase = sb("abase", [TA, 1])
        acol = sb("acol", [P, 3 * TA])
        aw_b = sb("aw_b", [P, 3, TA], bf16)
        aw_f = sb("aw_f", [P, 3, TA])
        khot = sb("khot", [P, 2, KEY], bf16)
        wlo = sb("wlo", [P, 2, 3, P], bf16)
        iota_k = sb("iota_k", [P, KEY], mybir.dt.float16)
        rown = sb("rown", [P, 1])
        rown2 = sb("rown2", [P, 1])
        roh = sb("roh", [P, 2 * P])
        M_sb = sb("M_sb", [P, D])
        tile_of = sb("tile_of", [TA, RA])
        slot_of = sb("slot_of", [P, 1])
        outs = sb("outs", [P, 2])
        tmm_i = sb("tmm_i", [NB, 2, TA], i32)
        tmm_f = sb("tmm_f", [NB, 2, TA])
        bmm_i = sb("bmm_i", [NB, 2], i32)
        bmm_s = sb("bmm_s", [NB, 2], i32)
        bmm_f = sb("bmm_f", [NB, 2])
        badf = sb("badf", [NB, 3])
        ones = sb("ones", [NB, P])
        nf_f = sb("nf_f", [1, 1])
        nf_i = sb("nf_i", [1, 1], i32)
        tio_i = arow_i
        iotak_i = node_sb[:, 0:KEY].bitcast(i32)
        slot_i = node_sb[:, KEY:KEY + RA].bitcast(i32)
        slot_f = node_sb[:, 2 * KEY:2 * KEY + RA]
        slot_m = node_sb[:, 3 * KEY:3 * KEY + RA]
        ln_s = sb("ln_s", [P, GB])
        ln_m = sb("ln_m", [P, GB])
        ln_v = sb("ln_v", [P, 2, GB])
        ln_r = sb("ln_r", [P, 2, GB])
        ln_q = sb("ln_q", [P, GB])
        eps_t = sb("eps_t", [P, 1])
        rc = sb("rc", [P, GB])
        tsum = sb("tsum", [P, GB * W])
        st = sb("st", [P, 16])
        bias = sb("bias", [P, 3])

        PS = ctx.enter_context(nc.psum_tensor("PS", [P, 8 * 512], f32))

        def bank(n, width, parts_n=P):
            return PS[0:parts_n, n * 512:n * 512 + width]

        bc_ps = [bank(0, GT * P), bank(2, GT * P)]
        u_ps = [bank(4, GT * W), bank(5, GT * W)]
        pw_ps = [PS[:, n * 512 + GT * W:n * 512 + GT * W + GT] for n in (4, 5)]
        win_ps = bank(6, 3 * D)
        A_ps = [bank(0, KH), bank(2, KH)]
        M_ps = bank(7, D, RA)
        aw_ps = PS[:, 7 * 512 + P:7 * 512 + 2 * P]
        aT_ps = PS[:, 6 * 512 + 384:6 * 512 + 384 + 3 * TA]
        ab_ps = PS[0:RA, 6 * 512 + 440:6 * 512 + 441]
        f_ps = bank(6, D)
        ptT_ps = PS[:, 6 * 512 + 444:6 * 512 + 508].bitcast(bf16)
        T_ps = [PS[:, j * 128:(j + 1) * 128] for j in range(GP)]
        T_all = PS[:, 0:GC]
        V_ps = [PS[:, 1024 + j * 128:1024 + (j + 1) * 128] for j in range(GP)]
        V_all = PS[:, 1024:1024 + GC]
        Z_ps = [bank(4, HALF), bank(5, HALF)]
        small_ps = bank(6, 8)

        s_in = sem("inputs_loaded")
        s_w = sem("weights_loaded")
        s_da = sem("dst_loaded")
        s_zero = sem("zeros_ready")
        s_iota = sem("iotas_ready")
        s_const = sem("constants_ready")
        s_sp = sem("spans_in_sbuf")
        s_spo = sem("spans_stored")
        s_spl = sem("spans_loaded")
        s_nw = sem("window_counts_ready")
        s_cum = sem("windows_summed")
        s_xc = sem("centred")
        s_sq = sem("squared")
        s_var = sem("variance_ready")
        s_std = sem("deviation_ready")
        s_h = sem("h_ready")
        s_hTp = sem("h_transposed")
        s_hTs = sem("h_transposed_in_sbuf")
        s_Hp = sem("h_table_product")
        s_Hs = sem("h_table_rows_in_sbuf")
        s_Ho = [sem("h_table_stored_even"), sem("h_table_stored_odd")]
        s_ldA = [sem("edges_loaded_even"), sem("edges_loaded_odd")]
        s_ldB = [sem("dst_weights_loaded_even"), sem("dst_weights_loaded_odd")]
        s_parts = sem("src_parts_ready")
        s_pT = sem("src_parts_transposed")
        s_pTs = sem("src_parts_transposed_in_sbuf")
        s_gidx = sem("gather_rows_ready")
        s_er = sem("edge_parts_rounded")
        s_ed = sem("edge_rests_ready")
        s_mr = sem("message_parts_rounded")
        s_md = sem("message_rests_ready")
        s_bc = sem("src_broadcast")
        s_M = sem("masks_ready")
        s_U = sem("duplicates_summed")
        s_Us = sem("sums_in_sbuf")
        s_sidx = sem("scatter_rows_ready")
        s_pace = sem("pool_passed_a_wait")
        s_free = sem("scatter_slots_free")
        s_g = [sem("gathered_even"), sem("gathered_odd")]
        s_tab = [sem(f"table_{k}_added") for k in range(K)]
        s_S = sem("window_one_hots_ready")
        s_Sm = sem("window_product")
        s_acc = sem("window_taken")
        s_win = sem("chunk_windows_done")
        s_al = sem("batch_loaded")
        s_ak = sem("batch_keys_ready")
        s_at = sem("batch_transposed")
        s_kh = sem("key_one_hots_ready")
        s_ap = sem("tile_weights_product")
        s_ke = sem("tile_weights_in_sbuf")
        s_Hd = sem("batch_rows_product")
        s_Ms = sem("batch_rows_in_sbuf")
        s_ro = sem("row_one_hots_ready")
        s_aw = sem("batch_product")
        s_fok = sem("extra_buffers_free")
        s_fl = sem("extra_edges_loaded")
        s_fg = sem("extra_gather_rows_ready")
        s_fd = sem("extra_gathered")
        s_fs = sem("extra_one_hots_ready")
        s_fm = sem("extra_product")
        s_rest = sem("first_pass_done")
        s_tg = [sem("table_group_loaded_even"), sem("table_group_loaded_odd")]
        s_v = sem("mean_edges_ready")
        s_vTp = sem("mean_edges_transposed")
        s_vTs = sem("mean_edges_transposed_in_sbuf")
        s_z = sem("layer_product")
        s_r = sem("layer_activated")
        s_sum = sem("layer_summed")
        s_tot = sem("layer_total")
        s_mean = sem("layer_mean")
        s_dev = sem("layer_deviations")
        s_vp = sem("layer_deviations_summed")
        s_vt = sem("layer_variance_total")
        s_vs = sem("layer_variance")
        s_sd = sem("layer_std")
        s_bn = sem("norm_ready")
        s_bp = sem("next_bias_product")
        s_wr = sem("next_weights_ready")
        s_b1 = sem("first_bias_ready")
        s_y = sem("normed_ready")
        s_yT = sem("normed_transposed")
        s_o = sem("out_rows_ready")
        s_out = [sem("out_stored_even"), sem("out_stored_odd")]

        block = ctx.enter_context(nc.Block())

        @block.sync
        def _(sp):
            def load_edges(c, q):
                rows = ds(c * P, P)
                sp.dma_start(src_i[:, q, :], src_v[rows, :]).then_inc(s_ldA[q], 16)
                sp.dma_start(gsrc_i[:, q, :], gsrc_v[rows, :]).then_inc(s_ldA[q], 16)
                sp.dma_start(ea_s[:, q, :], ea_v[rows, :]).then_inc(s_ldA[q], 16)

            def load_dst(c, q):
                rows = ds(c * P, P)
                sp.dma_start(dst_i[:, q, :], dst_v[rows, :]).then_inc(s_ldB[q], 16)
                sp.dma_start(ew_s[:, q, :], ew_v[rows, :]).then_inc(s_ldB[q], 16)

            load_edges(0, 0)
            load_edges(1, 1)
            sp.wait_ge(s_zero, 1)

            def load_x():
                sp.dma_start(X[:, 0:(B - 1) * D].rearrange("p (b d) -> p b d", d=D),
                             x[0:(B - 1) * P, :].rearrange("(b p) d -> p b d", p=P)).then_inc(s_in, 16)
                sp.dma_start(X[0:LAST, (B - 1) * D:B * D], x[(B - 1) * P:N, :]).then_inc(s_in, 16)

            load_x()
            for n, w in enumerate((w0, w1[0:D, :], w1[D:2 * D, :], w2, w3)):
                for o in (0, D):
                    sp.dma_start(Wd[o:o + D, n, o:o + D], w).then_inc(s_w, 16)
            with nc.allow_non_contiguous_dma(reason="columns of 64 values"):
                for n, v in enumerate((b1, b2, b3, g1, g2, g3, bt1, bt2, bt3)):
                    for o in (0, D):
                        sp.dma_start(vecs[o:o + D, n:n + 1], v.rearrange("(d o) -> d o", o=1)).then_inc(s_w, 16)
                sp.dma_start(gcol[:, :], gattr[0:1, :].rearrange("o d -> d o")).then_inc(s_w, 16)
            for o in (0, D):
                sp.dma_start(w1c[:, o:o + D], w1[2 * D:3 * D, :]).then_inc(s_w, 16)
            sp.dma_start(brow[:, :], b0.rearrange("(o d) -> o d", o=1).broadcast_to([P, D])).then_inc(s_w, 16)

            sp.dma_start(dst_all, dst_chunks).then_inc(s_da, 16)
            sp.dma_start(dst_rest[0:NB - 1, :], dst_batches).then_inc(s_da, 16)
            for h in range(2):
                sp.dma_start(dst_rest[NB - 1:NB, h * TL * P:(h + 1) * TL * P], dst_last).then_inc(s_da, 16)
            load_dst(0, 0)

            def load_batch(b):
                sp.wait_ge(s_ak, b + 1)
                for n in range(3):
                    sp.dma_start(arow_i[:, n, :], rest[n].bitcast(i32)[ds(b * TA, TA), :] if n == 2 else rest[n][ds(b * TA, TA), :]).then_inc(s_al, 16)

            load_batch(0)
            for i in range(NG):
                sp.wait_ge(s_Hs, i + 2)
                sp.dma_start(h_tab[:, i * GC:(i + 1) * GC], H[:, i * GC:(i + 1) * GC]).then_inc(s_Ho[i % 2], 16)

            sp.wait_ge(s_sp, 1)
            sp.dma_start(span_d, span_i[0:C, :]).then_inc(s_spo, 16)
            sp.dma_start(base_d, base_f[0:C, :]).then_inc(s_spo, 16)
            sp.wait_ge(s_spo, 32)
            sp.dma_start(spans[:, :], span_d.rearrange("(o c) f -> o (c f)", o=1)).then_inc(s_spl, 16)
            with nc.allow_non_contiguous_dma(reason="one row for all partitions"):
                sp.dma_start(bases[:, :], base_d.rearrange("(o c) f -> o (c f)", o=1).broadcast_to([P, 2 * C])).then_inc(s_spl, 16)

            def load_next(c, q):
                sp.wait_ge(s_sidx, c - 1)
                load_edges(c, q)
                sp.wait_ge(s_win, c)
                load_dst(c - 1, 1 - q)

            with sp.Fori(0, (C - 3) // 2) as i:
                load_next(2 * i + 2, 0)
                load_batch(i + 1)
                load_next(2 * i + 3, 1)
            load_next(C - 1, 0)
            sp.wait_ge(s_ak, NB)
            for n in range(3):
                for h in range(2):
                    last = rest[n][(NB - 1) * TA:NT, :]
                    sp.dma_start(arow_i[h * TL:(h + 1) * TL, n, :], last.bitcast(i32) if n == 2 else last).then_inc(s_al, 16)
            sp.wait_ge(s_win, C)
            load_dst(C - 1, 0)

            sp.wait_ge(s_zero, 2)
            load_x()

            sp.wait_ge(s_win, C + 2)
            extra = sp.value_load(nf_i[0:1, 0:1], min_val=0, max_val=C)
            with sp.If(extra > 0), sp.Fori(0, extra) as i:
                sp.wait_ge(s_fok, i + 1)
                rows = ds(i * P, P)
                for to, a in zip((gsrc_i, dst_i, ew_s), rest_f):
                    sp.dma_start(to[:, 0, 0:TF], a[rows, :]).then_inc(s_fl, 16)

            for k in range(K):
                sp.wait_ge(s_tab[k], 16 * G * C + 16)
            tabs = sum_tab.rearrange("(k r) d -> k (r d)", k=K)[:, 0:NPAD * W].rearrange("k (p n) -> p k n", p=P)

            def load_tables(i, q):
                for k in range(K):
                    sp.dma_start(tg[:, q, k, :], tabs[:, k, ds(i * GB * W, GB * W)]).then_inc(s_tg[q], 16)

            sp.wait_ge(s_rest, 1)
            load_tables(0, 0)
            load_tables(1, 1)
            with sp.Fori(0, (NG - 3) // 2) as i:
                sp.wait_ge(s_v, 2 * i + 1)
                load_tables(2 * i + 2, 0)
                sp.wait_ge(s_v, 2 * i + 2)
                load_tables(2 * i + 3, 1)
            sp.wait_ge(s_v, NG - 2)
            load_tables(NG - 1, 0)
            o_v = out[0:(B - 1) * P, :].rearrange("(b p) d -> p b d", p=P)
            for i in range(NG):
                sp.wait_ge(s_o, i + 1)
                rows = tg[:, i % 2, 0, 0:GC].rearrange("p (b d) -> p b d", d=D)
                nb = GB if i < NG - 1 else GB - 1
                sp.dma_start(o_v[:, i * GB:i * GB + nb, :], rows[:, 0:nb, :]).then_inc(s_out[i % 2], 16)
            sp.dma_start(out[(B - 1) * P:N, :], tg[0:LAST, (NG - 1) % 2, 0, GC - D:GC]).then_inc(s_out[(NG - 1) % 2], 16)
            sp.wait_ge(s_out[0], 16 * 5)
            sp.wait_ge(s_out[1], 16 * 3)

        @block.gpsimd
        def _(pool):
            nc.gpsimd.iota(iota_i[:, :], pattern=[[1, P]], base=0, channel_multiplier=0)
            nc.gpsimd.iota(pid_i[:, :], pattern=[[0, 1]], base=0, channel_multiplier=1)
            nc.gpsimd.iota(pw_i[:, :], pattern=[[0, 1]], base=190, channel_multiplier=-1)
            nc.gpsimd.iota(sel_i, pattern=[[1, T], [0, P]], base=0, channel_multiplier=0).then_inc(s_iota, 1)
            nc.gpsimd.iota(tio_i[:, 0, 0:RA].rearrange("p (t d) -> p t d", d=SPAN), pattern=[[1, TA], [0, SPAN]], base=0, channel_multiplier=0)
            nc.gpsimd.iota(slot_i[:, :], pattern=[[0, TA], [1, SPAN]], base=0, channel_multiplier=0)
            nc.gpsimd.iota(iotak_i[:, :], pattern=[[1, KEY]], base=0, channel_multiplier=0).then_inc(s_iota, 1)
            pool.wait_ge(s_zero, 1)
            for k in range(K):
                pool.dma_start(sum_tab[k * R:(k + 1) * R, :].rearrange("(p b) d -> p (b d)", p=P),
                               acc[:, :]).then_inc(s_tab[k], 16)

            def scatter(c, q, first=False):
                pool.wait_ge(s_sidx, c + 1)
                pool.wait_ge(s_Us, G * (c + 1) + 2)
                for t in range(T):
                    k, g = t % K, t // K
                    pool.wait_ge(s_tab[k], 16 * (G * c + g) + 16)
                    pool.sem_inc(s_pace, 1)
                    pool.indirect_dma_start(
                        out=sum_tab, out_offset=bass.IndirectOffsetOnAxis(ap=sidx[:, q, t:t + 1], axis=0),
                        in_=ust[:, q, t * W:(t + 1) * W], in_offset=None,
                        element_offset=k * R * W, compute_op=ALU.add).then_inc(s_tab[k], 16)
                    if t == K - 1 and not first:
                        pool.sem_inc(s_free, 1)

            def gather(c, q):
                pool.wait_ge(s_gidx, c + 1)
                pool.wait_ge(s_win, c + 1)
                pool.sem_inc(s_pace, 1)
                for t in range(TG):
                    pool.indirect_dma_start(
                        out=gat[:, q, t * D:(t + 1) * D], out_offset=None, in_=h_rows,
                        in_offset=bass.IndirectOffsetOnAxis(ap=gidx[:, q, t:t + 1], axis=0)).then_inc(s_g[q], 16)

            scatter(0, 0, first=True)
            scatter(1, 1)
            pool.wait_ge(s_nw, 1)
            pool.wait_ge(s_Ho[0], 16 * 4)
            pool.wait_ge(s_Ho[1], 16 * 3)
            gather(0, 0)
            gather(1, 1)
            with pool.Fori(0, (C - 3) // 2) as i:
                gather(2 * i + 2, 0)
                scatter(2 * i + 2, 0)
                gather(2 * i + 3, 1)
                scatter(2 * i + 3, 1)
            gather(C - 1, 0)
            scatter(C - 1, 0)
            extra = pool.value_load(nf_i[0:1, 0:1], min_val=0, max_val=C)
            with pool.If(extra > 0), pool.Fori(0, extra) as i:
                pool.wait_ge(s_fg, i + 1)
                pool.sem_inc(s_pace, 1)
                for t in range(TF):
                    pool.indirect_dma_start(
                        out=gat[:, 0, t * D:(t + 1) * D], out_offset=None, in_=h_rows,
                        in_offset=bass.IndirectOffsetOnAxis(ap=gidx[:, 0, t:t + 1], axis=0)).then_inc(s_fd, 16)

        @block.scalar
        def _(act):
            act.wait_ge(s_const, 1)

            def round_messages(c, q, k):
                act.wait_ge(s_md, 3 * c + k + 1)
                nc.scalar.copy(msg_p[:, :, k, :], gat[:, q, :].rearrange("p (t d) -> p t d", d=D)).then_inc(s_mr, 1)

            def stage(c, q, loads, messages=None):
                act.wait_ge(s_ldA[q], loads)
                for k in range(3):
                    if k:
                        act.wait_ge(s_ed, 2 * c + k)
                    nc.scalar.copy(ea_p[:, k, :, 0:D], ea_s[:, q, :].rearrange("p (t d) -> p t d", d=D)).then_inc(s_er, 1)
                act.wait_ge(s_free, c + 1)
                for g in range(G):
                    b = (q + g) % 2
                    if messages and g % 2 == 0:
                        round_messages(*messages, g // 2)
                    act.wait_ge(s_U, G * c + g + 3)
                    nc.scalar.copy(ust[:, q, g * GT * W:(g + 1) * GT * W], u_ps[b])
                    nc.scalar.copy(pw_s[:, g * GT:(g + 1) * GT], pw_ps[b]).then_inc(s_Us, 1)

            def square(n, q):
                act.wait_ge(s_xc, n + 1)
                nc.scalar.activation(sq[:, q, :], xc[:, q, :], ACT.Square).then_inc(s_sq, 1)

            def deviation(n, q):
                act.wait_ge(s_var, n + 1)
                nc.scalar.activation(ln_r[:, q, :], ln_v[:, q, :], ACT.Sqrt, bias=eps_t[:, :], scale=1.0 / D).then_inc(s_std, 1)

            def transposed_h(n):
                act.wait_ge(s_hTp, n + 1)
                nc.scalar.copy(hT[:, 0, :], T_all).then_inc(s_hTs, 1)

            def table_step(i, q):
                square(i + 1, 1 - q)
                deviation(i, q)
                transposed_h(i)

            stage(0, 0, 48)
            stage(1, 1, 48)
            square(0, 0)
            with act.Fori(0, (NG - 1) // 2) as i:
                table_step(2 * i, 0)
                table_step(2 * i + 1, 1)
            deviation(NG - 1, 0)
            transposed_h(NG - 1)

            def tile_weights(b, messages=None):
                for k in range(TA):
                    if messages and k % 3 == 0 and k < 9:
                        round_messages(*messages, k // 3)
                    for h in range(2):
                        act.wait_ge(s_ap, 2 * (TA * b + k) + h + 5)
                        nc.scalar.copy(A[:, k * KEY + h * KH:k * KEY + (h + 1) * KH], A_ps[h]).then_inc(s_ke, 1)

            def batch_rows(b):
                act.wait_ge(s_Hd, b + 1)
                nc.scalar.copy(M_sb[0:RA, :], M_ps).then_inc(s_Ms, 1)

            tile_weights(0, (0, 0))
            with act.Fori(0, (C - 3) // 2) as i:
                stage(2 * i + 2, 0, 48 * i + 96, (2 * i + 1, 1))
                stage(2 * i + 3, 1, 48 * i + 96)
                batch_rows(i)
                tile_weights(i + 1, (2 * i + 2, 0))
            stage(C - 1, 0, 48 * ((C + 1) // 2), (C - 2, 1))
            batch_rows(NB - 2)
            tile_weights(NB - 1)
            batch_rows(NB - 1)
            for k in range(3):
                round_messages(C - 1, 0, k)

            act.wait_ge(s_b1, 1)

            def first_layer(i):
                transposed_h(i + NG)
                act.wait_ge(s_vTp, i + 2)
                nc.scalar.copy(hT[:, 1, :], V_all).then_inc(s_vTs, 1)
                for h in range(2):
                    act.wait_ge(s_z, 2 * i + h + 1)
                    nc.scalar.activation(Rl[:, ds(i * GC + h * HALF, HALF)], Z_ps[h], ACT.Relu,
                                         bias=bias[:, 0:1]).then_inc(s_r, 1)

            square(NG, 0)
            with act.Fori(0, (NG - 1) // 2) as i:
                for q in range(2):
                    square(2 * i + q + NG + 1, 1 - q)
                    deviation(2 * i + q + NG, q)
                    first_layer(2 * i + q)
            deviation(2 * NG - 1, 0)
            first_layer(NG - 1)
            for n in range(3):
                if n:
                    act.wait_ge(s_wr, n)
                    with act.Fori(0, NG) as i:
                        for h in range(2):
                            act.wait_ge(s_z, 2 * NG * n + 2 * i + h + 1)
                            nc.scalar.activation(Rl[:, ds(i * GC + h * HALF, HALF)], Z_ps[h], ACT.Relu,
                                                 bias=bias[:, n:n + 1]).then_inc(s_r, 1)
                act.wait_ge(s_mean, n + 1)
                nc.scalar.activation(acc[:, 0:COLS - BAD], Rl[:, 0:COLS - BAD], ACT.Square, bias=st[:, 2:3],
                                     accum_out=st[:, 3:4])
                nc.scalar.activation(acc[0:D, COLS - BAD:COLS], Rl[0:D, COLS - BAD:COLS], ACT.Square,
                                     bias=st[0:D, 2:3], accum_out=st[0:D, 4:5]).then_inc(s_dev, 1)
                act.wait_ge(s_vs, n + 1)
                nc.scalar.activation(st[:, 7:8], st[:, 6:7], ACT.Sqrt, bias=eps_t[:, :], scale=1.0 / N).then_inc(s_sd, 1)

        @block.vector
        def _(dve):
            V = nc.vector

            def fence():
                V.drain()

            def by_block(a):
                return a.rearrange("p (b d) -> p b d", d=D)

            V.memset(acc[:, :], 0.0)
            V.memset(X[:, (B - 1) * D:B * D], 0.0)
            V.memset(Wd[:, :, :], 0.0)
            V.memset(ea_p[:, :, :, D:W], 0.0)
            fence()
            V.memset(ea_p[:, 0, :, D:W], 1.0)
            V.memset(st[:, :], 0.0)
            V.memset(base_f[:, :], 0.0)
            V.memset(parts[:, :], 0.0)
            V.memset(eps_t[:, :], EPS)
            V.drain().then_inc(s_zero, 1)
            V.memset(ones[:, :], 1.0)
            dve.wait_ge(s_iota, 2)
            V.tensor_copy(iota_f[:, :], iota_i[:, :])
            V.tensor_copy(iota_b[:, :], iota_i[:, :])
            V.tensor_copy(pid_f[:, :], pid_i[:, :])
            V.tensor_single_scalar(mod_i[:, :], iota_i[:, :], D - 1, ALU.bitwise_and)
            V.tensor_single_scalar(pmod_i[:, :], pid_i[:, :], D - 1, ALU.bitwise_and)
            V.tensor_single_scalar(pw_b[:, :], pw_i[:, :], 23, ALU.logical_shift_left)
            fence()
            V.tensor_copy(mod_f[:, :], mod_i[:, :])
            V.tensor_copy(pmod_f[:, :], pmod_i[:, :])
            V.tensor_scalar(kmod[:, :], pid_f[:, :], float(T), -float(T), ALU.is_ge, ALU.mult)
            V.tensor_scalar(spare_row[:, :], pid_f[:, :], float(NPAD), None, ALU.add)
            V.tensor_scalar(thr[:, :], pw_f, 2.5, None, ALU.mult)
            V.tensor_copy(pw_h[:, :], pw_f)
            V.tensor_scalar(ident[:, :], iota_f[:, :], pid_f[:, :], None, ALU.is_equal)
            V.tensor_scalar(ident_b[:, :], iota_f[:, :], pid_f[:, :], None, ALU.is_equal)
            V.tensor_scalar(before[:, :], iota_f[:, :], pid_f[:, :], None, ALU.is_gt)
            fence()
            V.tensor_tensor(kmod[:, :], kmod[:, :], pid_f[:, :], ALU.add)
            V.tensor_scalar(fold[:, :], mod_f[:, :], pmod_f[:, :], None, ALU.is_equal)
            fence()
            V.tensor_copy(iota_k[:, :], iotak_i)
            V.tensor_scalar(tile_of[:, :], tio_i[:, 0, 0:RA], pid_f[0:TA, :], None, ALU.is_equal)
            V.tensor_copy(slot_f, slot_i)
            V.tensor_scalar(slot_m, iota_f[:, 0:RA], pid_f[:, :], None, ALU.is_equal)
            V.tensor_scalar(outs[:, 1:2], pid_f[:, :], float(TL), OUTSIDE, ALU.is_ge, ALU.mult)
            fence()
            V.tensor_tensor(slot_m, slot_m, slot_f, ALU.mult)
            fence()
            V.tensor_reduce(slot_of[:, :], slot_m, AX.X, ALU.add)
            V.tensor_scalar(sel[:, :], sel_i, kmod[0:2 * T, :], None, ALU.is_equal)
            V.drain().then_inc(s_const, 1)
            V.drain().then_inc(s_U, 2)
            V.drain().then_inc(s_Us, 2)
            V.drain().then_inc(s_M, 2)
            V.drain().then_inc(s_free, 2)
            V.drain().then_inc(s_Sm, GG)
            V.drain().then_inc(s_ak, 1)
            V.drain().then_inc(s_ap, 4)
            V.drain().then_inc(s_ke, 2)
            V.drain().then_inc(s_fok, 1)
            V.drain().then_inc(s_fm, 1)
            V.drain().then_inc(s_acc, 1)
            V.drain().then_inc(s_win, 2)
            V.drain().then_inc(s_Hs, 1)
            V.drain().then_inc(s_vTp, 1)

            def centre(i, q, second=False):
                xg = X[:, ds(i * GC, GC)]
                if second:
                    V.tensor_tensor(xg, xg, acc[:, ds(i * GC, GC)], ALU.add)
                    fence()
                V.tensor_reduce(ln_s[:, :], by_block(xg), AX.X, ALU.add)
                fence()
                V.tensor_scalar(ln_m[:, :], ln_s[:, :], 1.0 / D, None, ALU.mult)
                fence()
                V.tensor_tensor(by_block(xc[:, q, :]), by_block(xg), ln_m[:, :].unsqueeze(2).broadcast_to([P, GB, D]),
                                ALU.subtract).then_inc(s_xc, 1)

            def normalise(n, q):
                dve.wait_ge(s_sq, n + 1)
                V.tensor_reduce(ln_v[:, q, :], by_block(sq[:, q, :]), AX.X, ALU.add).then_inc(s_var, 1)
                dve.wait_ge(s_std, n + 1)
                V.reciprocal(ln_q[:, :], ln_r[:, q, :])
                fence()
                V.scalar_tensor_tensor(out=by_block(hg[:, q, :]), in0=by_block(xc[:, q, :]), scalar=0.0,
                                       in1=ln_q[:, :].unsqueeze(2).broadcast_to([P, GB, D]),
                                       op0=ALU.max, op1=ALU.mult).then_inc(s_h, 1)

            def table_rows(i):
                dve.wait_ge(s_Hp, i + 1)
                V.tensor_tensor(by_block(H[:, i * GC:(i + 1) * GC]), by_block(V_all),
                                brow[:, :].unsqueeze(1).broadcast_to([P, GB, D]), ALU.add).then_inc(s_Hs, 1)

            def messages(c, q, pairs, k):
                rows = gat[:, q, :].rearrange("p (t d) -> p t d", d=D)
                if k:
                    dve.wait_ge(s_mr, 3 * c + k)
                    V.tensor_tensor(rows, rows, msg_p[:, :, k - 1, :], ALU.subtract).then_inc(s_md, 1)
                else:
                    dve.wait_ge(s_ldB[q], 32 * pairs)
                    dve.wait_ge(s_g[q], 16 * TG * pairs)
                    V.tensor_tensor(rows, rows, ew_s[:, q, :].unsqueeze(2).broadcast_to([P, TG, D]), ALU.mult).then_inc(s_md, 1)
                    V.tensor_copy(drel[:, :], dst_i[:, q, :])
                    fence()
                    V.tensor_scalar(drel[:, :], drel[:, :], bases[:, ds(2 * c, 1)], None, ALU.subtract)
                    fence()

            def gather_rows(q, n, ready):
                V.tensor_single_scalar(ghi_i[:, 0:n], gsrc_i[:, q, 0:n], 7, ALU.arith_shift_right)
                V.tensor_single_scalar(glo_i[:, 0:n], gsrc_i[:, q, 0:n], P - 1, ALU.bitwise_and)
                fence()
                V.tensor_copy(ghi_f[:, 0:n], ghi_i[:, 0:n])
                V.tensor_copy(glo_f[:, 0:n], glo_i[:, 0:n])
                fence()
                V.scalar_tensor_tensor(out=gidx[:, q, 0:n], in0=glo_f[:, 0:n], scalar=float(B), in1=ghi_f[:, 0:n],
                                       op0=ALU.mult, op1=ALU.add).then_inc(ready, 1)

            def prepare(c, q, loads, message_args=None):
                dve.wait_ge(s_ldA[q], loads)
                V.tensor_single_scalar(hi_i[:, :], src_i[:, q, :], 7, ALU.arith_shift_right)
                V.tensor_single_scalar(lo_i[:, :], src_i[:, q, :], P - 1, ALU.bitwise_and)
                fence()
                V.tensor_copy(hi_f[:, :], hi_i[:, :])
                V.tensor_copy(lo_f[:, :], lo_i[:, :])
                fence()
                V.tensor_scalar(parts[:, 0:T], hi_f[:, :], float(P), None, ALU.mult)
                V.tensor_copy(parts[:, T:2 * T], lo_f[:, :])
                V.scalar_tensor_tensor(out=src_f[:, :], in0=hi_f[:, :], scalar=float(P), in1=lo_f[:, :],
                                       op0=ALU.mult, op1=ALU.add)
                V.scalar_tensor_tensor(out=row_f[:, :], in0=lo_f[:, :], scalar=float(B), in1=hi_f[:, :],
                                       op0=ALU.mult, op1=ALU.add)
                V.drain().then_inc(s_parts, 1)
                gather_rows(q, TG, s_gidx)
                rest_of = ea_s[:, q, :].rearrange("p (t d) -> p t d", d=D)
                for k in range(2):
                    dve.wait_ge(s_er, 3 * c + k + 1)
                    V.tensor_tensor(rest_of, rest_of, ea_p[:, k, :, 0:D], ALU.subtract).then_inc(s_ed, 1)
                dve.wait_ge(s_pT, c + 1)
                V.tensor_copy(partsT[:, :], ptT_ps[0:2 * T, :]).then_inc(s_pTs, 1)
                for g in range(G):
                    b = (q + g) % 2
                    n = G * c + g
                    if message_args and g % 2 == 0:
                        messages(*message_args, g // 2)
                    dve.wait_ge(s_bc, n + 1)
                    dve.wait_ge(s_U, n + 1)
                    V.tensor_tensor(Mt[:, b, :].rearrange("p (t i) -> p t i", i=P),
                                    bc_ps[b].rearrange("p (t i) -> p t i", i=P),
                                    src_f[:, g * GT:(g + 1) * GT].unsqueeze(2).broadcast_to([P, GT, P]),
                                    ALU.is_equal).then_inc(s_M, 1)
                dve.wait_ge(s_Us, G * (c + 1) + 2)
                V.tensor_scalar(flag[:, :], pw_s[:, :], thr[:, :], None, ALU.is_lt)
                V.tensor_scalar(row_f[:, :], row_f[:, :], spare_row[:, :], None, ALU.subtract)
                fence()
                V.tensor_tensor(row_f[:, :], row_f[:, :], flag[:, :], ALU.mult)
                fence()
                dve.wait_ge(s_free, c + 1)
                V.tensor_scalar(sidx[:, q, :], row_f[:, :], spare_row[:, :], None, ALU.add).then_inc(s_sidx, 1)

            def windows(c):
                first = dve.value_load(spans[0:1, ds(4 * c, 1)], min_val=0, max_val=B - 1)
                count = dve.value_load(spans[0:1, ds(4 * c + 1, 1)], min_val=1, max_val=B)
                done = dve.value_load(spans[0:1, ds(4 * c + 2, 1)], min_val=0, max_val=B * C)
                with dve.Fori(0, count) as j:
                    for g in range(GG):
                        dve.wait_ge(s_Sm, (done + j) * GG + g + 1)
                        V.tensor_tensor(St[:, g, :].rearrange("p (t i) -> p t i", i=P),
                                        iota_b[:, :].unsqueeze(1).broadcast_to([P, GTG, P]),
                                        drel[:, g * GTG:(g + 1) * GTG].unsqueeze(2).broadcast_to([P, GTG, P]),
                                        ALU.is_equal).then_inc(s_S, 1)
                    dve.wait_ge(s_Sm, (done + j) * GG + 2 * GG)
                    V.tensor_scalar(drel[:, :], drel[:, :], float(P), None, ALU.subtract)
                    a = acc[:, ds(nc.s_assert_within(first + j, min_val=0, max_val=B - 1) * D, D)]
                    V.tensor_reduce(wsum[:, :], win_ps.rearrange("p (k d) -> p d k", k=3), AX.X, ALU.add).then_inc(s_acc, 1)
                    fence()
                    V.tensor_tensor(a, a, wsum[:, :], ALU.add)
                    fence()
                V.drain().then_inc(s_win, 1)

            prepare(0, 0, 48)
            prepare(1, 1, 48)

            dve.wait_ge(s_da, 64)
            V.tensor_reduce(mm_i[0:C, 0:1], dst_all, AX.X, ALU.min)
            V.tensor_reduce(mm_i[0:C, 1:2], dst_all, AX.X, ALU.max)
            fence()
            V.tensor_single_scalar(mm_s[0:C, :], mm_i[0:C, :], 7, ALU.arith_shift_right)
            V.memset(span_f[0:C, 3:4], 0.0)
            fence()
            V.tensor_copy(span_f[0:C, 0:1], mm_s[0:C, 0:1])
            V.tensor_copy(mm_f[0:C, :], mm_s[0:C, 1:2])
            fence()
            V.scalar_tensor_tensor(out=span_f[0:C, 1:2], in0=mm_f[0:C, :], scalar=1.0, in1=span_f[0:C, 0:1],
                                   op0=ALU.add, op1=ALU.subtract)
            V.tensor_scalar(base_f[0:C, 0:1], span_f[0:C, 0:1], float(P), None, ALU.mult)
            tiles_rest = dst_rest.rearrange("b (t e) -> b t e", e=P)
            V.tensor_reduce(tmm_i[:, 0, :], tiles_rest, AX.X, ALU.min)
            V.tensor_reduce(tmm_i[:, 1, :], tiles_rest, AX.X, ALU.max)
            fence()
            V.tensor_copy(tmm_f[:, :, :], tmm_i[:, :, :])
            V.tensor_reduce(bmm_i[:, 0:1], tmm_i[:, 0, :], AX.X, ALU.min)
            V.tensor_reduce(bmm_i[:, 1:2], tmm_i[:, 1, :], AX.X, ALU.max)
            fence()
            V.tensor_single_scalar(bmm_s[:, :], bmm_i[:, :], 7, ALU.arith_shift_right)
            V.tensor_tensor(tmm_f[:, 1, :], tmm_f[:, 1, :], tmm_f[:, 0, :], ALU.subtract)
            fence()
            V.tensor_copy(bmm_f[:, :], bmm_s[:, :])
            V.tensor_reduce(badf[:, 0:1], tmm_f[:, 1, :], AX.X, ALU.max)
            fence()
            V.tensor_scalar(span_f[0:NB, 3:4], bmm_f[:, 0:1], float(B - 2), None, ALU.min)
            V.tensor_scalar(badf[:, 0:1], badf[:, 0:1], float(SPAN) - 0.5, None, ALU.is_gt)
            fence()
            V.tensor_scalar(base_f[0:NB, 1:2], span_f[0:NB, 3:4], float(P), None, ALU.mult)
            V.tensor_tensor(badf[:, 1:2], bmm_f[:, 1:2], span_f[0:NB, 3:4], ALU.subtract)
            fence()
            V.tensor_scalar(badf[:, 1:2], badf[:, 1:2], 1.5, None, ALU.is_gt)
            fence()
            V.tensor_tensor(badf[:, 2:3], badf[:, 0:1], badf[:, 1:2], ALU.add)
            V.drain().then_inc(s_nw, 1)
            dve.wait_ge(s_in, 32)
            centre(0, 0)
            for i in range(NG):
                if i + 1 < NG:
                    centre(i + 1, (i + 1) % 2)
                normalise(i, i % 2)
                if i:
                    table_rows(i - 1)
            table_rows(NG - 1)

            dve.wait_ge(s_w, 16 * 32)
            dve.wait_ge(s_cum, 1)
            V.tensor_copy(span_f[0:C, 2:3], small_ps[0:C, 0:1])
            V.tensor_scalar(outs[:, 0:1], small_ps[:, 6:7], 0.5, OUTSIDE, ALU.is_gt, ALU.mult)
            V.tensor_scalar(nf_f[:, :], small_ps[0:1, 6:7], 0.5, float(C), ALU.is_gt, ALU.mult)
            fence()
            V.tensor_tensor(outs[:, 1:2], outs[:, 1:2], outs[:, 0:1], ALU.add)
            V.tensor_copy(nf_i[:, :], nf_f[:, :])
            V.tensor_tensor(bias[:, 0:1], small_ps[:, 1:2], vecs[:, 0:1], ALU.add).then_inc(s_b1, 1)
            fence()
            V.tensor_copy(span_i[0:C, :], span_f[0:C, :]).then_inc(s_sp, 1)

            dve.wait_ge(s_spl, 32)
            def batch(b, out_col=0, loads=None, message_args=None, before=None):
                dve.wait_ge(s_al, 48 * b + 48 if loads is None else loads)
                V.tensor_reduce(abase_i[:, :], arow_i[:, 1, :], AX.X, ALU.min)
                V.tensor_single_scalar(ahl_i[:, 0, :], arow_i[:, 0, :], 7, ALU.arith_shift_right)
                V.tensor_single_scalar(ahl_i[:, 1, :], arow_i[:, 0, :], P - 1, ALU.bitwise_and)
                V.tensor_copy(arow[:, 0, :], arow_i[:, 1, :])
                V.tensor_copy(arow[:, 2, :], arow_i[:, 2, :].bitcast(f32))
                fence()
                V.tensor_copy(abase[:, :], abase_i[:, :])
                V.tensor_copy(arow[:, 1, :], ahl_i[:, 1, :])
                fence()
                V.tensor_scalar(arow[:, 0, :], arow[:, 0, :], abase[:, :], float(B), ALU.subtract, ALU.mult)
                fence()
                V.tensor_scalar(arow[:, 0, :], arow[:, 0, :], outs[0:TA, out_col:out_col + 1], None, ALU.add)
                fence()
                V.tensor_tensor(arow[:, 0, :], arow[:, 0, :], ahl_i[:, 0, :], ALU.add).then_inc(s_ak, 1)
                dve.wait_ge(s_at, b + 1)
                V.tensor_copy(acol[:, :], aT_ps)
                V.tensor_tensor(rown[0:RA, :], ab_ps, slot_of[0:RA, :], ALU.add)
                fence()
                w = acol[:, 2 * TA:3 * TA]
                V.tensor_scalar(rown[0:RA, :], rown[0:RA, :], bases[0:RA, ds(2 * b + 1, 1)], None, ALU.subtract)
                V.tensor_copy(aw_b[:, 0, :], w)
                fence()
                V.tensor_copy(aw_f[:, 0, :], aw_b[:, 0, :])
                V.tensor_scalar(rown2[0:RA, :], rown[0:RA, :], float(P), None, ALU.subtract)
                fence()
                V.tensor_tensor(w, w, aw_f[:, 0, :], ALU.subtract)
                fence()
                V.tensor_copy(aw_b[:, 1, :], w)
                fence()
                V.tensor_copy(aw_f[:, 1, :], aw_b[:, 1, :])
                fence()
                V.tensor_tensor(aw_f[:, 2, :], w, aw_f[:, 1, :], ALU.subtract)
                fence()
                for k in range(TA):
                    if message_args and k % 3 == 0 and k < 9:
                        messages(*message_args, k // 3)
                    dve.wait_ge(s_ap, 2 * (TA * b + k) + 2)
                    V.tensor_scalar(khot[:, k % 2, :], iota_k[:, :], acol[:, k:k + 1], None, ALU.is_equal)
                    for n in range(3):
                        last = V.tensor_scalar(wlo[:, k % 2, n, :], iota_b[:, :], acol[:, TA + k:TA + k + 1],
                                               aw_f[:, n, k:k + 1], ALU.is_equal, ALU.mult)
                    last.then_inc(s_kh, 1)
                    if k == 1:
                        if before is not None:
                            add_batch(before)
                        V.tensor_scalar(roh[0:RA, 0:P], iota_f[0:RA, :], rown[0:RA, :], None, ALU.is_equal)
                        V.tensor_scalar(roh[0:RA, P:2 * P], iota_f[0:RA, :], rown2[0:RA, :], None, ALU.is_equal).then_inc(s_ro, 1)

            def add_batch(b):
                block = dve.value_load(spans[0:1, ds(4 * b + 3, 1)], min_val=0, max_val=B - 2)
                dve.wait_ge(s_aw, b + 1)
                a = acc[:, ds(block * D, 2 * D)]
                V.tensor_tensor(a, a, aw_ps, ALU.add)
                fence()

            batch(0, message_args=(0, 0, 1))
            with dve.Fori(0, (C - 3) // 2) as i:
                windows(2 * i)
                prepare(2 * i + 2, 0, 48 * i + 96, (2 * i + 1, 1, i + 1))
                windows(2 * i + 1)
                prepare(2 * i + 3, 1, 48 * i + 96)
                batch(i + 1, message_args=(2 * i + 2, 0, i + 2), before=i)
            windows(C - 3)
            prepare(C - 1, 0, 48 * ((C + 1) // 2), (C - 2, 1, (C - 1) // 2))
            add_batch(NB - 2)
            windows(C - 2)
            batch(NB - 1, 1, 48 * (NB + 1))
            add_batch(NB - 1)
            V.memset(X[:, (B - 1) * D:B * D], 0.0)
            V.drain().then_inc(s_zero, 1)
            for k in range(3):
                messages(C - 1, 0, (C + 1) // 2, k)
            windows(C - 1)

            extra = dve.value_load(nf_i[0:1, 0:1], min_val=0, max_val=C)
            with dve.If(extra > 0), dve.Fori(0, extra) as i:
                dve.wait_ge(s_fl, 48 * i + 48)
                gather_rows(0, TF, s_fg)
                dve.wait_ge(s_fd, 16 * TF * i + 16 * TF)
                rows = gat[:, 0, 0:TF * D].rearrange("p (t d) -> p t d", d=D)
                V.tensor_tensor(rows, rows, ew_s[:, 0, 0:TF].unsqueeze(2).broadcast_to([P, TF, D]), ALU.mult)
                V.tensor_copy(drel[:, 0:TF], dst_i[:, 0, 0:TF])
                fence()
                with dve.Fori(0, B) as j:
                    dve.wait_ge(s_fm, i * B + j + 1)
                    V.tensor_tensor(Sf.rearrange("p (t i) -> p t i", i=P), iota_f[:, :].unsqueeze(1).broadcast_to([P, TF, P]),
                                    drel[:, 0:TF].unsqueeze(2).broadcast_to([P, TF, P]), ALU.is_equal).then_inc(s_fs, 1)
                    dve.wait_ge(s_fm, i * B + j + 2)
                    V.tensor_scalar(drel[:, 0:TF], drel[:, 0:TF], float(P), None, ALU.subtract)
                    a = acc[:, ds(j * D, D)]
                    V.tensor_tensor(a, a, f_ps, ALU.add)
                    fence()
                V.drain().then_inc(s_fok, 1)
            V.drain().then_inc(s_rest, 1)


            def mean_edges(i, q, loads):
                dve.wait_ge(s_tg[q], 16 * K * loads)
                V.tensor_tensor(tsum[:, :], tg[:, q, 0, :], tg[:, q, 1, :], ALU.add)
                for k in range(2, K):
                    fence()
                    V.tensor_tensor(tsum[:, :], tsum[:, :], tg[:, q, k, :], ALU.add)
                fence()
                dve.wait_ge(s_vTp, i + 1)
                sums = tsum[:, :].rearrange("p (b w) -> p b w", w=W)
                V.tensor_scalar(rc[:, :], sums[:, :, D], 1.0, None, ALU.max)
                fence()
                V.reciprocal(rc[:, :], rc[:, :])
                fence()
                V.tensor_tensor(by_block(ve[:, :]), sums[:, :, 0:D],
                                rc[:, :].unsqueeze(2).broadcast_to([P, GB, D]), ALU.mult).then_inc(s_v, 1)

            fence()
            dve.wait_ge(s_in, 64)
            centre(0, 0, second=True)
            with dve.Fori(0, (NG - 1) // 2) as i:
                for q in range(2):
                    n = 2 * i + q
                    centre(n + 1, 1 - q, second=True)
                    dve.wait_ge(s_hTp, NG + n - 1)
                    normalise(NG + n, q)
                    mean_edges(n, q, i + 1)
            normalise(2 * NG - 1, 0)
            mean_edges(NG - 1, 0, (NG + 1) // 2)

            for n in range(3):
                dve.wait_ge(s_r, 2 * NG * (n + 1))
                V.memset(Rl[D:P, COLS - BAD:COLS], 0.0)
                fence()
                V.tensor_reduce(st[:, 0:1], Rl[:, :], AX.X, ALU.add).then_inc(s_sum, 1)
                dve.wait_ge(s_tot, n + 1)
                V.tensor_scalar(st[:, 1:2], small_ps[:, 2:3], 1.0 / N, None, ALU.mult)
                V.tensor_scalar(st[:, 2:3], small_ps[:, 2:3], -1.0 / N, None, ALU.mult).then_inc(s_mean, 1)
                dve.wait_ge(s_dev, n + 1)
                V.tensor_tensor(st[:, 5:6], st[:, 3:4], st[:, 4:5], ALU.add).then_inc(s_vp, 1)
                dve.wait_ge(s_vt, n + 1)
                V.tensor_copy(st[:, 6:7], small_ps[:, 3:4]).then_inc(s_vs, 1)
                dve.wait_ge(s_sd, n + 1)
                V.reciprocal(st[:, 8:9], st[:, 7:8])
                fence()
                V.tensor_tensor(st[:, 9:10], st[:, 8:9], vecs[:, 3 + n:4 + n], ALU.mult)
                fence()
                V.tensor_tensor(st[:, 10:11], st[:, 9:10], st[:, 1:2], ALU.mult)
                fence()
                V.tensor_tensor(st[:, 11:12], vecs[:, 6 + n:7 + n], st[:, 10:11], ALU.subtract).then_inc(s_bn, 1)
                if n < 2:
                    V.tensor_scalar(Ws[:, :], Wd[:, 3 + n, :], st[:, 9:10], None, ALU.mult)
                    dve.wait_ge(s_bp, n + 1)
                    V.tensor_tensor(bias[:, n + 1:n + 2], small_ps[:, 4:5], vecs[:, n + 1:n + 2], ALU.add).then_inc(s_wr, 1)
            fence()
            for i in range(NG):
                V.tensor_scalar(hg[:, i % 2, :], Rl[:, i * GC:(i + 1) * GC], st[:, 9:10], st[:, 11:12],
                                ALU.mult, ALU.add).then_inc(s_y, 1)
                dve.wait_ge(s_yT, i + 1)
                if i >= 2:
                    dve.wait_ge(s_out[i % 2], 16 * (i // 2))
                V.tensor_tensor(tg[:, i % 2, 0, 0:GC], X[:, i * GC:(i + 1) * GC], T_all, ALU.add).then_inc(s_o, 1)

        @block.tensor
        def _(pe):
            mm = nc.tensor.matmul

            pe.wait_ge(s_const, 1)

            def transpose_h(q):
                for j in range(GP):
                    last = nc.tensor.transpose(T_ps[j], hg[:, q, j * P:(j + 1) * P], ident[:, :])
                return last

            def table_product(i, q):
                pe.wait_ge(s_h, i + 1)
                transpose_h(q).then_inc(s_hTp, 1)
                pe.wait_ge(s_hTs, i + 1)
                pe.wait_ge(s_Hs, i + 1)
                for j in range(GP):
                    last = mm(V_ps[j], hT[:, 0, j * P:(j + 1) * P], Wd[:, 0, :], start=True, stop=True)
                last.then_inc(s_Hp, 1)

            def broadcast(c, q, g):
                b = (q + g) % 2
                pe.wait_ge(s_M, G * c + g + 1)
                for j in range(GT):
                    t = g * GT + j
                    last = mm(bc_ps[b][:, j * P:(j + 1) * P], sel[:, t * P:(t + 1) * P], partsT[:, :], start=True, stop=True)
                last.then_inc(s_bc, 1)

            def prepare(c, q, rows=None):
                pe.wait_ge(s_parts, c + 1)
                nc.tensor.transpose(ptT_ps, parts[:, :], ident_b[:, :]).then_inc(s_pT, 1)
                pe.wait_ge(s_pTs, c + 1)
                broadcast(c, q, 0)
                broadcast(c, q, 1)
                for g in range(G):
                    b = (q + g) % 2
                    n = G * c + g
                    pe.wait_ge(s_M, n + 3)
                    pe.wait_ge(s_Us, n + 1)
                    if g == 0:
                        pe.wait_ge(s_er, 3 * c + 3)
                    for j in range(GT):
                        t = g * GT + j
                        mask = Mt[:, b, j * P:(j + 1) * P]
                        for k in range(3):
                            mm(u_ps[b][:, j * W:(j + 1) * W], mask, ea_p[:, k, t, :], start=(k == 0), stop=(k == 2))
                        last = mm(pw_ps[b][:, j:j + 1], mask, pw_h[:, :], start=True, stop=True)
                    last.then_inc(s_U, 1)
                    if g + 2 < G:
                        broadcast(c, q, g + 2)
                    if rows:
                        batch_rows(rows[0], *rows[1 + g:3 + g])

            def windows(c, q):
                count = pe.value_load(spans[0:1, ds(4 * c + 1, 1)], min_val=1, max_val=B)
                pe.wait_ge(s_mr, 3 * c + 3)
                done = pe.value_load(spans[0:1, ds(4 * c + 2, 1)], min_val=0, max_val=B * C)
                with pe.Fori(0, count) as j:
                    pe.wait_ge(s_acc, done + j + 1)
                    for g in range(GG):
                        pe.wait_ge(s_S, (done + j) * GG + g + 1)
                        for t in range(GTG):
                            e = g * GTG + t
                            last = mm(win_ps, St[:, g, t * P:(t + 1) * P], msg_p[:, e, :, :],
                                      start=(e == 0), stop=(e == TG - 1))
                        last.then_inc(s_Sm, 1)

            prepare(0, 0)
            prepare(1, 1)

            pe.wait_ge(s_w, 16 * 32)
            with pe.Fori(0, (NG - 1) // 2) as i:
                table_product(2 * i, 0)
                table_product(2 * i + 1, 1)
            table_product(NG - 1, 0)

            pe.wait_ge(s_nw, 1)
            mm(small_ps[0:C, 0:1], before[0:C, 0:C], span_f[0:C, 1:2], start=True, stop=True)
            mm(small_ps[:, 6:7], ones[:, :], badf[:, 2:3], start=True, stop=True)
            mm(small_ps[:, 1:2], w1c[:, :], gcol[:, :], start=True, stop=True).then_inc(s_cum, 1)

            pe.wait_ge(s_spl, 32)
            def batch(b, before=None):
                pe.wait_ge(s_ak, b + 2)
                mm(ab_ps, tile_of[:, :], abase[:, :], start=True, stop=True)
                for n in range(3):
                    last = nc.tensor.transpose(aT_ps[:, n * TA:(n + 1) * TA], arow[:, n, :], ident[0:TA, 0:TA])
                last.then_inc(s_at, 1)
                if before is not None:
                    batch_rows(before, cuts[1][-1], B)
                    batch_sum(before)
                for k in range(TA):
                    pe.wait_ge(s_kh, TA * b + k + 1)
                    for h in range(2):
                        pe.wait_ge(s_ke, 2 * (TA * b + k) + h + 1)
                        for n in range(3):
                            last = mm(A_ps[h], wlo[:, k % 2, n, :], khot[:, k % 2, h * KH:(h + 1) * KH], start=(n == 0), stop=(n == 2))
                        last.then_inc(s_ap, 1)

            def batch_rows(b, h0, h1):
                for h in range(h0, h1):
                    last = mm(M_ps, A_rows[:, :, h], H[:, h * D:(h + 1) * D], start=(h == 0), stop=(h == B - 1))
                if h1 == B:
                    last.then_inc(s_Hd, 1)

            def batch_sum(b):
                pe.wait_ge(s_ro, b + 1)
                pe.wait_ge(s_Ms, b + 1)
                mm(aw_ps[:, 0:D], roh[0:RA, 0:P], M_sb[0:RA, :], start=True, stop=True)
                mm(aw_ps[:, D:2 * D], roh[0:RA, P:2 * P], M_sb[0:RA, :], start=True, stop=True).then_inc(s_aw, 1)

            cuts = [[0, 16, 43, 44, 45, 46, 47, 48], [48, 55, 82, 83, 84, 85, 86, 87]]

            def step(b, c, q, half):
                n = cuts[half]
                batch_rows(b, n[0], n[1])
                windows(c, q)
                batch_rows(b, n[1], n[2])
                prepare(c + 2, q, [b] + n[2:])

            batch(0)
            with pe.Fori(0, (C - 3) // 2) as i:
                pe.wait_ge(s_ke, 2 * TA * (i + 1) + 2)
                step(i, 2 * i, 0, 0)
                step(i, 2 * i + 1, 1, 1)
                batch(i + 1, i)
            pe.wait_ge(s_ke, 2 * TA * (NB - 1) + 2)
            step(NB - 2, C - 3, 0, 0)
            batch_rows(NB - 2, cuts[1][0], B)
            batch_sum(NB - 2)
            windows(C - 2, 1)
            batch(NB - 1)
            pe.wait_ge(s_ke, 2 * TA * NB + 2)
            batch_rows(NB - 1, 0, B)
            batch_sum(NB - 1)
            windows(C - 1, 0)

            extra = pe.value_load(nf_i[0:1, 0:1], min_val=0, max_val=C)
            with pe.If(extra > 0), pe.Fori(0, extra) as i:
                with pe.Fori(0, B) as j:
                    pe.wait_ge(s_fs, i * B + j + 1)
                    for t in range(TF):
                        last = mm(f_ps, Sf[:, t * P:(t + 1) * P], gat[:, 0, t * D:(t + 1) * D], start=(t == 0), stop=(t == TF - 1))
                    last.then_inc(s_fm, 1)

            def first_layer(i, q):
                pe.wait_ge(s_h, NG + i + 1)
                transpose_h(q).then_inc(s_hTp, 1)
                pe.wait_ge(s_v, i + 1)
                for j in range(GP):
                    last = nc.tensor.transpose(V_ps[j], ve[:, j * P:(j + 1) * P], ident[:, :])
                last.then_inc(s_vTp, 1)
                pe.wait_ge(s_hTs, NG + i + 1)
                pe.wait_ge(s_vTs, i + 1)
                for h in range(2):
                    cols = slice(h * HALF, (h + 1) * HALF)
                    mm(Z_ps[h], Wd[:, 1, :], hT[:, 0, cols], start=True, stop=False)
                    mm(Z_ps[h], Wd[:, 2, :], hT[:, 1, cols], start=False, stop=True).then_inc(s_z, 1)

            with pe.Fori(0, (NG - 1) // 2) as i:
                first_layer(2 * i, 0)
                first_layer(2 * i + 1, 1)
            first_layer(NG - 1, 0)
            for n in range(3):
                if n:
                    pe.wait_ge(s_wr, n)
                    with pe.Fori(0, NG) as i:
                        for h in range(2):
                            pe.wait_ge(s_r, 2 * NG * n + 2 * i + h - 1)
                            mm(Z_ps[h], Ws[:, :], Rl[:, ds(i * GC + h * HALF, HALF)], start=True, stop=True).then_inc(s_z, 1)
                pe.wait_ge(s_sum, n + 1)
                mm(small_ps[:, 2:3], fold[:, :], st[:, 0:1], start=True, stop=True).then_inc(s_tot, 1)
                pe.wait_ge(s_vp, n + 1)
                mm(small_ps[:, 3:4], fold[:, :], st[:, 5:6], start=True, stop=True).then_inc(s_vt, 1)
                if n < 2:
                    pe.wait_ge(s_bn, n + 1)
                    mm(small_ps[:, 4:5], Wd[:, 3 + n, :], st[:, 11:12], start=True, stop=True).then_inc(s_bp, 1)
            for i in range(NG):
                pe.wait_ge(s_y, i + 1)
                transpose_h(i % 2).then_inc(s_yT, 1)


_INS = ["x", "src", "dst", "edge_attr_64", "edge_weight", "L0_gnn_W", "L0_gnn_b", "L1_gnn_global_attr",
        "L1_gnn_W1", "L1_gnn_b1", "L1_gnn_W2", "L1_gnn_b2", "L1_gnn_W3", "L1_gnn_b3",
        "L1_gnn_g1", "L1_gnn_bt1", "L1_gnn_g2", "L1_gnn_bt2", "L1_gnn_g3", "L1_gnn_bt3"]


def kernel(**inputs):
    import numpy as np
    import concourse.bacc as bacc
    from concourse.bass_utils import run_bass_kernel_spmd

    nc = bacc.Bacc("TRN2", target_bir_lowering=False, num_devices=1)
    arrays, args = {}, []
    for name in _INS:
        a = np.ascontiguousarray(inputs[name])
        arrays[f"in_{name}"] = a
        args.append(nc.dram_tensor(f"in_{name}", a.shape, mybir.dt.from_np(a.dtype), kind="ExternalInput").ap())
    out = nc.dram_tensor("out_0", (N, D), mybir.dt.float32, kind="ExternalOutput").ap()
    gnn_kernel(nc, *args, out)
    r = run_bass_kernel_spmd(nc, [arrays], core_ids=[0])
    return r.results[0]["out_0"]
```
